# Optimizing a Trainium2 kernel written in Bass

```python
import numpy as np
import jax
import jax.numpy as jnp

def _softmax(x, axis=-1):
    return jax.nn.softmax(x, axis=axis)

def _gelu(x):
    return jax.nn.gelu(x, approximate=True)

def _silu(x):
    return jax.nn.silu(x)

def _sigmoid(x):
    return jax.nn.sigmoid(x)

def _layernorm(x, axis=-1, eps=1e-05):
    m = jnp.mean(x, axis=axis, keepdims=True)
    v = jnp.var(x, axis=axis, keepdims=True)
    return (x - m) / jnp.sqrt(v + eps)

def _scatter_add(tgt, idx, src, axis=0):
    return tgt.at[idx].add(src)

def _segment_sum(src, seg, n):
    return jax.ops.segment_sum(src, seg, n)
kernel_name = 'mk_seq_preln_d2_jaxref_r8_1a2240'

def setup_inputs(seed: int=0):
    np.random.seed(seed)
    _w = jnp.asarray

    def _L0_attn_setup():
        import jax, jax.numpy as jnp
        import numpy as np
        DIM = 128
        HEADS = 16
        DIM_HEAD = 64
        SOFTCLAMP = 50.0

        def _rmsnorm(x, w):
            eps = jnp.finfo(x.dtype).eps
            var = jnp.mean(jnp.square(x), axis=-1, keepdims=True)
            return x * jax.lax.rsqrt(var + eps) * w

        def _head_rmsnorm(x, gamma):
            norm = jnp.linalg.norm(x, axis=-1, keepdims=True)
            normed = x / jnp.maximum(norm, 1e-12)
            scale = (gamma + 1.0) * DIM_HEAD ** 0.5
            return normed * scale[None, :, None, :]
        key = jax.random.key(seed)
        ks = jax.random.split(key, 7)
        b, n = (4, 256)
        di = HEADS * DIM_HEAD
        s = 0.02
        return {'tokens': jax.random.normal(ks[0], (b, n, DIM), dtype=jnp.float32), 'norm_w': jnp.ones((DIM,), dtype=jnp.float32), 'Wq': jax.random.normal(ks[1], (DIM, di), dtype=jnp.float32) * s, 'Wkv': jax.random.normal(ks[2], (DIM, 2 * di), dtype=jnp.float32) * s, 'Wo': jax.random.normal(ks[3], (di, DIM), dtype=jnp.float32) * s, 'q_gamma': jnp.zeros((HEADS, DIM_HEAD), dtype=jnp.float32), 'k_gamma': jnp.zeros((HEADS, DIM_HEAD), dtype=jnp.float32)}
    _L0_attn_in = _L0_attn_setup()

    def _L0_ffn_setup():
        import jax, jax.numpy as jnp
        import numpy as np
        D_MODEL = 128
        NUM_HEADS = 4
        NUM_EXPERTS = 8
        TOP_K = 2
        D_FF = 128
        EPS = 1e-06

        def _rmsnorm(x, g):
            return x * jax.lax.rsqrt(jnp.mean(x * x, axis=-1, keepdims=True) + EPS) * g

        def _swiglu(x, w1, w2, w3):
            return jax.nn.silu(x @ w1.T) * (x @ w3.T) @ w2.T
        key = jax.random.key(seed)
        ks = jax.random.split(key, 16)
        d, e, f = (D_MODEL, NUM_EXPERTS, D_FF)
        dc = d // 4
        s = 0.02
        return {'X': jax.random.normal(ks[0], (2, 128, d), dtype=jnp.float32), 'g1': jnp.ones((d,), jnp.float32), 'g2': jnp.ones((d,), jnp.float32), 'Wq': jax.random.normal(ks[1], (d, d), jnp.float32) * s, 'Wkc': jax.random.normal(ks[2], (dc, d), jnp.float32) * s, 'Wvc': jax.random.normal(ks[3], (dc, d), jnp.float32) * s, 'Wo': jax.random.normal(ks[4], (d, d), jnp.float32) * s, 'Wr': jax.random.normal(ks[5], (e, d), jnp.float32) * s, 'expert_bias': jnp.zeros((e,), jnp.float32), 'sW1': jax.random.normal(ks[6], (f, d), jnp.float32) * s, 'sW2': jax.random.normal(ks[7], (d, f), jnp.float32) * s, 'sW3': jax.random.normal(ks[8], (f, d), jnp.float32) * s, 'eW1': jax.random.normal(ks[9], (e, f, d), jnp.float32) * s, 'eW2': jax.random.normal(ks[10], (e, d, f), jnp.float32) * s, 'eW3': jax.random.normal(ks[11], (e, f, d), jnp.float32) * s}
    _L0_ffn_in = _L0_ffn_setup()

    def _L1_attn_setup():
        import jax, jax.numpy as jnp
        import numpy as np
        BASE_THETA = 0.5
        K_DOP = 0.2
        K_NOR = 0.15
        K_SERO = 0.1
        DIM = 128
        key = jax.random.key(seed)
        ks = jax.random.split(key, 9)
        scale = 1.0 / np.sqrt(DIM)
        x = jax.random.normal(ks[0], (2, 256, DIM), dtype=jnp.float32)
        Wq = jax.random.normal(ks[1], (DIM, DIM), dtype=jnp.float32) * scale
        bq = jnp.zeros((DIM,), dtype=jnp.float32)
        Wk = jax.random.normal(ks[2], (DIM, DIM), dtype=jnp.float32) * scale
        bk = jnp.zeros((DIM,), dtype=jnp.float32)
        Wv = jax.random.normal(ks[3], (DIM, DIM), dtype=jnp.float32) * scale
        bv = jnp.zeros((DIM,), dtype=jnp.float32)
        Wo = jax.random.normal(ks[4], (DIM, DIM), dtype=jnp.float32) * scale
        bo = jnp.zeros((DIM,), dtype=jnp.float32)
        return {'x': x, 'Wq': Wq, 'bq': bq, 'Wk': Wk, 'bk': bk, 'Wv': Wv, 'bv': bv, 'Wo': Wo, 'bo': bo}
    _L1_attn_in = _L1_attn_setup()

    def _L1_ffn_setup():
        import jax, jax.numpy as jnp
        import numpy as np
        B, T, C = (4, 256, 128)
        E, F, K = (8, 256, 2)
        key = jax.random.key(seed)
        k0, k1, k2, k3 = jax.random.split(key, 4)
        s = lambda d: 1.0 / np.sqrt(d)
        x = jax.random.normal(k0, (B, T, C), dtype=jnp.float32)
        Wr = jax.random.normal(k1, (E, C), dtype=jnp.float32) * s(C)
        W1 = jax.random.normal(k2, (E, 2 * F, C), dtype=jnp.float32) * s(C)
        W2 = jax.random.normal(k3, (E, C, F), dtype=jnp.float32) * s(F)
        return {'x': x, 'Wr': Wr, 'W1': W1, 'W2': W2}
    _L1_ffn_in = _L1_ffn_setup()
    _d = {'L0_attn_tokens': _L0_attn_in['tokens'], 'L0_attn_norm_w': _L0_attn_in['norm_w'], 'L0_attn_Wq': _L0_attn_in['Wq'], 'L0_attn_Wkv': _L0_attn_in['Wkv'], 'L0_attn_Wo': _L0_attn_in['Wo'], 'L0_attn_q_gamma': _L0_attn_in['q_gamma'], 'L0_attn_k_gamma': _L0_attn_in['k_gamma'], 'L0_ffn_g1': _L0_ffn_in['g1'], 'L0_ffn_g2': _L0_ffn_in['g2'], 'L0_ffn_Wq': _L0_ffn_in['Wq'], 'L0_ffn_Wkc': _L0_ffn_in['Wkc'], 'L0_ffn_Wvc': _L0_ffn_in['Wvc'], 'L0_ffn_Wo': _L0_ffn_in['Wo'], 'L0_ffn_Wr': _L0_ffn_in['Wr'], 'L0_ffn_expert_bias': _L0_ffn_in['expert_bias'], 'L0_ffn_sW1': _L0_ffn_in['sW1'], 'L0_ffn_sW2': _L0_ffn_in['sW2'], 'L0_ffn_sW3': _L0_ffn_in['sW3'], 'L0_ffn_eW1': _L0_ffn_in['eW1'], 'L0_ffn_eW2': _L0_ffn_in['eW2'], 'L0_ffn_eW3': _L0_ffn_in['eW3'], 'L1_attn_Wq': _L1_attn_in['Wq'], 'L1_attn_bq': _L1_attn_in['bq'], 'L1_attn_Wk': _L1_attn_in['Wk'], 'L1_attn_bk': _L1_attn_in['bk'], 'L1_attn_Wv': _L1_attn_in['Wv'], 'L1_attn_bv': _L1_attn_in['bv'], 'L1_attn_Wo': _L1_attn_in['Wo'], 'L1_attn_bo': _L1_attn_in['bo'], 'L1_ffn_Wr': _L1_ffn_in['Wr'], 'L1_ffn_W1': _L1_ffn_in['W1'], 'L1_ffn_W2': _L1_ffn_in['W2']}
    _x0 = _d['L0_attn_tokens']
    _d['L0_attn_tokens'] = jax.random.normal(jax.random.fold_in(jax.random.key(seed), 1), (32, 256, 128), dtype=_x0.dtype)
    del _x0
    return _d

def reference(L0_attn_tokens, L0_attn_norm_w, L0_attn_Wq, L0_attn_Wkv, L0_attn_Wo, L0_attn_q_gamma, L0_attn_k_gamma, L0_ffn_g1, L0_ffn_g2, L0_ffn_Wq, L0_ffn_Wkc, L0_ffn_Wvc, L0_ffn_Wo, L0_ffn_Wr, L0_ffn_expert_bias, L0_ffn_sW1, L0_ffn_sW2, L0_ffn_sW3, L0_ffn_eW1, L0_ffn_eW2, L0_ffn_eW3, L1_attn_Wq, L1_attn_bq, L1_attn_Wk, L1_attn_bk, L1_attn_Wv, L1_attn_bv, L1_attn_Wo, L1_attn_bo, L1_ffn_Wr, L1_ffn_W1, L1_ffn_W2):

    def _L0_attn_ref(tokens, norm_w, Wq, Wkv, Wo, q_gamma, k_gamma):
        import jax, jax.numpy as jnp
        import numpy as np
        DIM = 128
        HEADS = 16
        DIM_HEAD = 64
        SOFTCLAMP = 50.0

        def _rmsnorm(x, w):
            eps = jnp.finfo(x.dtype).eps
            var = jnp.mean(jnp.square(x), axis=-1, keepdims=True)
            return x * jax.lax.rsqrt(var + eps) * w

        def _head_rmsnorm(x, gamma):
            norm = jnp.linalg.norm(x, axis=-1, keepdims=True)
            normed = x / jnp.maximum(norm, 1e-12)
            scale = (gamma + 1.0) * DIM_HEAD ** 0.5
            return normed * scale[None, :, None, :]
        b, n, _ = tokens.shape
        x = _rmsnorm(tokens, norm_w)
        q = x @ Wq
        kv = x @ Wkv
        k, v = jnp.split(kv, 2, axis=-1)
        split = lambda t: t.reshape(b, n, HEADS, DIM_HEAD).transpose(0, 2, 1, 3)
        q, k, v = (split(q), split(k), split(v))
        q = _head_rmsnorm(q, q_gamma)
        k = _head_rmsnorm(k, k_gamma)
        sim = jnp.einsum('bhid,bhjd->bhij', q, k)
        sim = jnp.tanh(sim / SOFTCLAMP) * SOFTCLAMP
        sim = sim * DIM_HEAD ** (-0.5)
        attn = jax.nn.softmax(sim, axis=-1)
        out = jnp.einsum('bhij,bhjd->bhid', attn, v)
        out = out.transpose(0, 2, 1, 3).reshape(b, n, HEADS * DIM_HEAD)
        return out @ Wo

    def _L0_ffn_ref(X, g1, g2, Wq, Wkc, Wvc, Wo, Wr, expert_bias, sW1, sW2, sW3, eW1, eW2, eW3):
        import jax, jax.numpy as jnp
        import numpy as np
        D_MODEL = 128
        NUM_HEADS = 4
        NUM_EXPERTS = 8
        TOP_K = 2
        D_FF = 128
        EPS = 1e-06

        def _rmsnorm(x, g):
            return x * jax.lax.rsqrt(jnp.mean(x * x, axis=-1, keepdims=True) + EPS) * g

        def _swiglu(x, w1, w2, w3):
            return jax.nn.silu(x @ w1.T) * (x @ w3.T) @ w2.T
        B, S, d = X.shape
        H = NUM_HEADS
        dk = d // H
        scale = 1.0 / jnp.sqrt(jnp.float32(dk))
        nx = _rmsnorm(X, g1)
        Q = (nx @ Wq.T).reshape(B, S, H, dk).transpose(0, 2, 1, 3)
        Kc = nx @ Wkc.T
        Vc = nx @ Wvc.T
        scores = jnp.einsum('bhsd,btd->bhst', Q, Kc) * scale
        attn = jax.nn.softmax(scores, axis=-1)
        out = jnp.einsum('bhst,btd->bhsd', attn, Vc)
        out = out.transpose(0, 2, 1, 3).reshape(B, S, d) @ Wo.T
        X = X + out
        nx = _rmsnorm(X, g2)
        xf = nx.reshape(-1, d)
        logits = xf @ Wr.T + expert_bias
        rw = jax.nn.softmax(logits, axis=-1)
        topw, topi = jax.lax.top_k(rw, TOP_K)
        topw = jax.nn.softmax(topw, axis=-1)
        combine = jnp.sum(jax.nn.one_hot(topi, NUM_EXPERTS, dtype=xf.dtype) * topw[..., None], axis=1)
        shared = _swiglu(xf, sW1, sW2, sW3)
        h = jax.nn.silu(jnp.einsum('td,efd->etf', xf, eW1)) * jnp.einsum('td,efd->etf', xf, eW3)
        eo = jnp.einsum('etf,edf->etd', h, eW2)
        specialist = jnp.einsum('te,etd->td', combine, eo)
        moe_out = (shared + specialist).reshape(B, S, d)
        return X + moe_out

    def _L1_attn_ref(x, Wq, bq, Wk, bk, Wv, bv, Wo, bo):
        import jax, jax.numpy as jnp
        import numpy as np
        BASE_THETA = 0.5
        K_DOP = 0.2
        K_NOR = 0.15
        K_SERO = 0.1
        DIM = 128
        q = jnp.einsum('bsd,ed->bse', x, Wq) + bq
        k = jnp.einsum('bsd,ed->bse', x, Wk) + bk
        v = jnp.einsum('bsd,ed->bse', x, Wv) + bv
        qk = jnp.einsum('bsd,btd->bst', q, k)
        theta = BASE_THETA + K_DOP * jax.nn.sigmoid(qk) + K_NOR * jnp.tanh(qk) + K_SERO * jax.nn.relu(qk)
        attn = jax.nn.softmax(theta, axis=-1)
        out = jnp.einsum('bst,btd->bsd', attn, v)
        return jnp.einsum('bsd,ed->bse', out, Wo) + bo

    def _L1_ffn_ref(x, Wr, W1, W2):
        import jax, jax.numpy as jnp
        import numpy as np
        B, T, C = (4, 256, 128)
        E, F, K = (8, 256, 2)
        Bb, Tt, Cc = x.shape
        flat = x.reshape(-1, Cc)
        N = flat.shape[0]
        logits = flat @ Wr.T
        weights, ids = jax.lax.top_k(logits, K)
        weights = jax.nn.softmax(weights, axis=-1)
        rows = jnp.arange(N)[:, None]
        router_weights = jnp.zeros((N, E), dtype=flat.dtype).at[rows, ids].add(weights)
        h = jnp.einsum('nc,efc->nef', flat, W1)
        val, gate = (h[..., :F], h[..., F:])
        act = val * jax.nn.silu(gate)
        expert_outputs = jnp.einsum('nef,ecf->nec', act, W2)
        out = jnp.einsum('nec,ne->nc', expert_outputs, router_weights)
        return out.reshape(Bb, Tt, Cc)
    x = L0_attn_tokens
    x = x + _L0_attn_ref(_layernorm(x, axis=-1), L0_attn_norm_w, L0_attn_Wq, L0_attn_Wkv, L0_attn_Wo, L0_attn_q_gamma, L0_attn_k_gamma)
    x = x + _L0_ffn_ref(_layernorm(x, axis=-1), L0_ffn_g1, L0_ffn_g2, L0_ffn_Wq, L0_ffn_Wkc, L0_ffn_Wvc, L0_ffn_Wo, L0_ffn_Wr, L0_ffn_expert_bias, L0_ffn_sW1, L0_ffn_sW2, L0_ffn_sW3, L0_ffn_eW1, L0_ffn_eW2, L0_ffn_eW3)
    x = x + _L1_attn_ref(_layernorm(x, axis=-1), L1_attn_Wq, L1_attn_bq, L1_attn_Wk, L1_attn_bk, L1_attn_Wv, L1_attn_bv, L1_attn_Wo, L1_attn_bo)
    x = x + _L1_ffn_ref(_layernorm(x, axis=-1), L1_ffn_Wr, L1_ffn_W1, L1_ffn_W2)
    return x

_drawn_inputs = setup_inputs


def setup_inputs(seed=0):
    import zlib

    import numpy as np

    out = dict(_drawn_inputs(seed))
    spreads = {'L0_attn_norm_w': (1.0, 0.6),
     'L0_attn_q_gamma': (0.0, 0.8),
     'L0_attn_k_gamma': (0.0, 0.8),
     'L0_ffn_g1': (1.0, 0.6),
     'L0_ffn_g2': (1.0, 0.6),
     'L0_ffn_expert_bias': (0.0, 0.8),
     'L1_attn_bq': (0.0, 2.0),
     'L1_attn_bk': (0.0, 2.0),
     'L1_attn_bv': (0.0, 0.757),
     'L1_attn_bo': (0.0, 0.785)}
    factors = {'L0_ffn_Wq': 8.0,
     'L0_ffn_Wkc': 8.0,
     'L0_ffn_Wvc': 8.0,
     'L0_ffn_Wo': 8.0,
     'L0_ffn_Wr': 8.0,
     'L0_ffn_sW1': 7.639,
     'L0_ffn_sW2': 7.257,
     'L0_ffn_sW3': 7.832,
     'L0_ffn_eW1': 8.0,
     'L0_ffn_eW2': 8.0,
     'L0_ffn_eW3': 8.0,
     'L1_attn_Wq': 3.787,
     'L1_attn_Wk': 3.376}
    for name, (base, spread) in spreads.items():
        noise = np.random.default_rng([zlib.crc32(name.encode()), seed]).standard_normal(out[name].shape)
        drawn = base * np.exp(spread * noise) if base else spread * noise
        out[name] = jnp.asarray(drawn.astype(out[name].dtype))
    for name, factor in factors.items():
        out[name] = (out[name] * factor).astype(out[name].dtype)
    return out
```

```python
from contextlib import ExitStack

import concourse.bass as bass
from concourse import mybir
from concourse.alu_op_type import AluOpType as ALU

F32 = mybir.dt.float32
F32R = mybir.dt.float32r
U32 = mybir.dt.uint32
ACT = mybir.ActivationFunctionType
AX_X = mybir.AxisListType.X

P = 128
D = 128
SEQ = 256
T = 4
N = T * P
H, DH = 16, 64
HP = H // 2
INNER = H * DH
CLAMP = 50.0
FH, FD = 4, 32
E0, E1 = 8, 8
J1 = 2
LN_EPS = 1e-5
RMS0_EPS = 1.1920928955078125e-07
RMS1_EPS = 1e-6

C_QK = 0
C_V = C_QK + 2 * INNER
C_FQ = C_V + INNER
C_FK = C_FQ + D
C_FV = C_FK + FH * FD
C_F1 = C_FV + FD
C_F3 = C_F1 + (E0 + 1) * D
C_FR = C_F3 + (E0 + 1) * D
C_LQ = C_FR + E0
C_LK = C_LQ + D
C_LV = C_LK + D
C_LR = C_LV + D
C_L1 = C_LR + E1
C_RSPLIT = C_L1 + E1 * 4 * D
C_WO = 0
C_FWO = C_WO + HP * D
C_F2 = C_FWO + D
C_LWO = C_F2 + (E0 + 1) * D
C_L2 = C_LWO + D
C_PLAIN = C_L2 + E1 * J1 * D
V_NW, V_G1, V_G2, V_BQ, V_BK, V_QG = 0, 1, 2, 3, 4, 5
V_KG = V_QG + HP
V_EB = V_KG + HP
V_BV = V_EB + E0
V_BO = V_BV + D
C_VEC = V_BO + D

GROUPS = [(C_QK, C_FQ, V_NW), (C_FQ, C_F1, V_G1), (C_F1, C_LQ, V_G2), (C_LQ, C_L1, None), (C_L1, C_RSPLIT, None)]


HALF = HP // 2


def a_head(b):
    steps = [("a_qk", (b, 0, 0), 2.0), ("a_qk", (b, 0, 1), 2.0), ("a_qk", (b, 1, 0), 2.0), ("a_scale", (b, 0, 0), 0.2),
             ("a_qk", (b, 1, 1), 2.0), ("a_scale", (b, 0, 1), 0.2)]
    steps += [("a_v", (2 * b,), 2.0), ("a_scale", (b, 1, 0), 0.2), ("a_v", (2 * b + 1,), 2.0), ("a_pairs", (b, 0, 0), 1.5),
              ("a_scale", (b, 1, 1), 0.2), ("a_pairs", (b, 0, 1), 1.5), ("a_pairs", (b, 1, 0), 1.5),
              ("a_pairs", (b, 1, 1), 1.5)]
    return steps


def a_body(b):
    g0 = b * HP
    steps = [("a_scores", (g0,), 1.8), ("a_scores", (g0 + 1,), 1.8)]
    for g in range(g0, g0 + HP):
        if g + 2 < g0 + HP:
            steps.append(("a_scores", (g + 2,), 1.8))
        steps.append(("a_values", (g,), 1.8))
        if g == g0 + HP - 3:
            steps.append(("a_norm", (1 - b,), 0.0, b))
    return steps + [("a_turn", (1 - b,), 0.5, b), ("a_turn_out", (2 * b,), 1.0), ("a_turn_out", (2 * b + 1,), 1.5),
                    ("a_out", (b,), 3.5)]


def b_second_attention():
    steps = [("f_turn_x", (), 1.5), ("f_project", (), 3.0)]
    for t in range(T):
        steps += [("f_scores", (t,), 4.0), ("f_turn", (t,), 1.5), ("f_values", (t,), 1.7)]
    return steps + [("f_turn_out", (), 1.5), ("f_out", (), 1.5), ("f_norm", (), 2.5)]


def b_third_attention():
    return [("l_norm", (), 2.0), ("l_turn_x", (), 1.5), ("l_project", (), 3.0), ("l_scores", (), 6.0),
            ("l_turn", (), 2.0), ("l_values", (), 3.0), ("l_turn_out", (), 1.5), ("l_out", (), 1.5),
            ("l_norm2", (), 2.0)]


def b_mixture(m, experts, parts):
    steps = [("m_turn_x", (m,), 1.5), ("m_router", (m,), 1.5), ("m_up", (m, 0), 1.5), ("m_top_a", (m,), 1.0)]
    for s in range(1, experts * parts):
        steps.append(("m_up", (m, s), 1.5))
        if s == 1:
            steps.append(("m_top_b", (m,), 1.0))
        if s == 2:
            steps.append(("m_top_c", (m,), 1.0))
        if s % parts == 0:
            steps.append(("m_down", (m, s // parts - 1), 0.9 * parts))
        if m and s == 8:
            steps.append(("b_norm", (), 1.0, 1))
    steps.append(("m_down", (m, experts - 1), 0.9 * parts))
    return steps


def merged(*streams):
    placed = []
    for offset, steps in streams:
        total, at = sum(s[2] for s in steps), 0.0
        for n, (name, args, w, *ahead) in enumerate(steps):
            placed.append((at / total, offset, n, name, args, sum(ahead)))
            at += w
    return [(offset + ahead, name, args) for _, offset, n, name, args, ahead in sorted(placed)]


M0_STEPS, M1_STEPS = b_mixture(0, E0 + 1, 1), b_mixture(1, E1, J1)
FIRST = ([(0, "a_norm", (0,)), (0, "a_turn", (0,))] + merged((0, a_head(0))) + merged((0, a_body(0)))
         + merged((0, a_head(1))) + merged((0, a_body(1))) + [(0, "b_norm", ())] + merged((1, a_head(0))))
EARLY = (merged((1, a_body(0)), (0, b_second_attention())) + merged((1, a_head(1)), (0, M0_STEPS))
         + merged((1, a_body(1)), (0, b_third_attention())))
PASS = EARLY + merged((2, a_head(0)), (0, M1_STEPS))
LAST_BUT_ONE = [step for step in EARLY + merged((0, M1_STEPS)) if step[0] < 2]
LAST = [step for part in (b_second_attention(), M0_STEPS, b_third_attention(), M1_STEPS)
        for step in merged((0, part)) if step[0] < 1]
CHAIN_A, CHAIN_X, CHAIN_B, CHAIN_N = 24, 6, 41, 2


def program(nc, x, wr, wf, vec, out):
    UNITS = x.shape[0] * x.shape[1] // N
    assert UNITS > 2
    x_u = x.rearrange("b s d -> (b s) d").rearrange("(u t p) d -> u p t d", t=T, p=P)
    out_u = out.rearrange("b s d -> (b s) d").rearrange("(u t p) d -> u p t d", t=T, p=P)

    with ExitStack() as ctx:
        def sb(name, shape, dt=F32):
            return ctx.enter_context(nc.sbuf_tensor(name, shape, dt))

        def semaphore(name):
            return ctx.enter_context(nc.semaphore(name))

        class Signal:

            def __init__(self, name, per_unit, before=0):
                self.sem = semaphore(name)
                self.per_unit, self.before, self.links = per_unit, before, 0

            def at(self, i, k):
                return i * self.per_unit + (k + self.before)

        WH = sb("WH", [P, C_RSPLIT], F32R)
        WL = sb("WL", [P, C_RSPLIT], F32R)
        WF = sb("WF", [P, C_PLAIN])
        VEC = sb("VEC", [P, C_VEC])
        gamma = sb("gamma", [P, HP])
        ident = sb("ident", [P, P])
        half_neg = sb("half_neg", [P, 2 * H])
        iota8 = sb("iota8", [P, 8])
        A_COLS, B_COLS = 8192, 6144
        arena = sb("arena", [P, A_COLS + B_COLS])
        stage = arena[:, 0:C_RSPLIT]

        raw = arena[:, 0:4096].rearrange("p (t n) -> p t n", t=2)
        ao = raw[:, :, 0:INNER]
        aoT = raw[:, :, INNER:2 * INNER]
        qT = arena[:, 4096:6144].rearrange("p (j n) -> p j n", j=HP)
        kT = arena[:, 6144:8192].rearrange("p (j n) -> p j n", j=HP)
        pT = sb("pT", [P, 3, 2, 2, SEQ])
        sq = pT[:, 0:2, :, :, :].rearrange("p a b c d -> p a (b c d)")
        vx = sb("vx", [P, 2, H, DH + 1])
        xin = sb("xin", [P, T, D])
        xn_a = sb("xn_a", [P, 2, D])
        xTh_a = sb("xTh_a", [P, SEQ], F32R)
        xTl_a = sb("xTl_a", [P, SEQ], F32R)
        stats_a = sb("stats_a", [P, 2, 6])
        mv_a = sb("mv_a", [P, 2, 2])
        parg_a = sb("parg_a", [P, 2])
        prs_a = sb("prs_a", [P, 2])
        ss = sb("ss", [P, 2, 2 * H])
        rn = sb("rn", [P, 2, 2 * H])
        rd_a = sb("rd_a", [P, 2, 4])
        xa = sb("xa", [P, T, D])

        def region(base, size):
            assert base + size <= B_COLS
            return arena[:, A_COLS + base:A_COLS + base + size]

        xr = sb("xr", [P, T, D])
        xl = sb("xl", [P, T, D])
        xn = sb("xn", [P, T, D])
        xTh = sb("xTh", [P, N], F32R)
        xTl = sb("xTl", [P, N], F32R)
        stats = sb("stats", [P, T, 6])
        mv = sb("mv", [P, T, 2])
        parg = sb("parg", [P, 2, T])
        prs = sb("prs", [P, 2, T])
        ms = sb("ms", [P, T])
        touch_a = sb("touch_a", [P, 2])
        touch_b = sb("touch_b", [P, 2])
        rd = sb("rd", [P, 4])
        nm = sb("nm", [P, 2, 4])
        idx8 = sb("idx8", [P, T, 8], U32)
        comb = sb("comb", [P, T, 8])
        fqz = sb("fqz", [P, FH, N])
        fv = sb("fv", [P, T, FD + 1])
        lv = sb("lv", [P, T, D + 1])
        fk = region(0, N)
        fp = region(512, 1024).rearrange("p (h k) -> p h k", h=FH)
        fpT = region(1536, 1024).rearrange("p (m q) -> p m q", m=2 * FH)
        fo = region(2560, N).rearrange("p (t d) -> p t d", t=T)
        foT = region(3072, N)
        lq, lk = region(0, N), region(512, N)
        ltheta = region(1024, 2 * N).rearrange("p (b n) -> p b n", b=2)
        lth, lth2 = region(2048, N), region(2560, N)
        lp = region(3072, 2 * N).rearrange("p (t k) -> p t k", t=T)
        lpT = region(4096, 2 * N).rearrange("p (b m q) -> p b m q", b=2, m=4)
        lo = region(5120, N).rearrange("p (t d) -> p t d", t=T)
        loT = region(5632, N)
        th = region(0, 2 * N).rearrange("p (s n) -> p s n", s=2)
        gated = region(1024, 2 * N).rearrange("p (s n) -> p s n", s=2)
        hid = region(2048, 4 * N).rearrange("p (s n) -> p s n", s=4)
        small = region(4096, 12 * T * 8).rearrange("p (k n) -> p k n", k=12)

        PS = ctx.enter_context(nc.psum_tensor("PS", [P, 8, 512], F32))

        def bank(b, n=512):
            return PS[:, b, 0:n]

        def banks(b, k):
            return PS[:, b:b + k, :].rearrange("p b n -> p (b n)")

        SHARED, A_OUT, B_ONE, B_TWO = 2, 4, 5, 6

        setup_dma = [semaphore(f"setup_dma{k}") for k in range(len(GROUPS) + 2)]
        ident_zero = semaphore("ident_zero")
        fqz_zero = semaphore("fqz_zero")
        ident_ready = semaphore("ident_ready")
        weights_hi = semaphore("weights_hi")
        weights_ready = semaphore("weights_ready")
        consts_ready = semaphore("consts_ready")
        x_loaded = Signal("x_loaded", 32)
        x_stored = Signal("x_stored", 16, before=16)
        chain_a = Signal("chain_a", CHAIN_A)
        chain_x = Signal("chain_x", CHAIN_X)
        chain_b = Signal("chain_b", CHAIN_B)
        chain_n = Signal("chain_n", CHAIN_N)
        a_pow_arg = Signal("a_pow_arg", 2)
        a_pow_done = Signal("a_pow_done", 2)
        a_xn = Signal("a_xn", 2)
        a_xT_psum = Signal("a_xT_psum", 2)
        a_xT = Signal("a_xT", 2)
        qk_psum = Signal("qk_psum", 2 * T)
        v_psum = Signal("v_psum", T)
        raw_copied = Signal("raw_copied", 2 * T)
        v_copied = Signal("v_copied", T)
        squared = Signal("squared", 2 * T)
        ss_ready = Signal("ss_ready", 2 * T)
        rn_ready = Signal("rn_ready", 2 * T)
        qk_normed = Signal("qk_normed", 2 * T)
        pairs_psum = Signal("pairs_psum", 8)
        qT_ready = Signal("qT_ready", 4)
        kT_ready = Signal("kT_ready", 4)
        s_psum = Signal("s_psum", 2 * HP)
        tanh_done = Signal("tanh_done", 2 * HP)
        p_ready = Signal("p_ready", 2 * HP)
        o_psum = Signal("o_psum", 2 * HP)
        o_normed = Signal("o_normed", 2 * HP)
        aoT_psum = Signal("aoT_psum", T)
        aoT_act = Signal("aoT_act", T)
        aoT_dve = Signal("aoT_dve", T)
        wo_psum = Signal("wo_psum", 2)
        x_added = Signal("x_added", 2)
        b_pow_arg = Signal("b_pow_arg", 4)
        b_pow_done = Signal("b_pow_done", 4)
        b_xn = Signal("b_xn", 4)
        b_xT_psum = Signal("b_xT_psum", 4)
        b_xT = Signal("b_xT", 4)
        f_proj = Signal("f_proj", 3)
        fq_ready = Signal("fq_ready", 1)
        fk_ready = Signal("fk_ready", 1)
        fv_ready = Signal("fv_ready", 1)
        f_scores_psum = Signal("f_scores_psum", T)
        f_max = Signal("f_max", T)
        f_p = Signal("f_p", T)
        f_pT_psum = Signal("f_pT_psum", T)
        f_pT_act = Signal("f_pT_act", T)
        f_pT_dve = Signal("f_pT_dve", T)
        f_o_psum = Signal("f_o_psum", T)
        f_o = Signal("f_o", T)
        f_oT_psum = Signal("f_oT_psum", 1)
        f_oT = Signal("f_oT", 1)
        f_wo = Signal("f_wo", 1)
        x2_ready = Signal("x2_ready", 1, before=1)
        x2_squares = Signal("x2_squares", 1)
        l_proj = Signal("l_proj", 3)
        lqk_ready = Signal("lqk_ready", 2)
        lv_ready = Signal("lv_ready", 1)
        l_scores_psum = Signal("l_scores_psum", 2)
        l_maps = Signal("l_maps", 2)
        l_theta = Signal("l_theta", 2)
        l_max = Signal("l_max", 2)
        l_p = Signal("l_p", 2)
        l_pT_psum = Signal("l_pT_psum", 2)
        l_pT_dve = Signal("l_pT_dve", 1)
        l_pT_act = Signal("l_pT_act", 1)
        l_o_psum = Signal("l_o_psum", 2)
        l_o = Signal("l_o", 2)
        l_oT_psum = Signal("l_oT_psum", 1)
        l_oT = Signal("l_oT", 1)
        l_wo = Signal("l_wo", 1)
        l_x = Signal("l_x", 1)
        l_xb = Signal("l_xb", 1)

        class Mixture:

            def __init__(self, tag, experts, parts, gate_col, value_col, down_col, router_col, shared, norm):
                self.experts, self.parts, self.shared, self.norm = experts, parts, shared, norm
                self.steps = experts * parts
                self.gate_col, self.value_col, self.down_col, self.router_col = gate_col, value_col, down_col, router_col
                self.router_psum = Signal(f"{tag}_router_psum", 1)
                self.logits_read = Signal(f"{tag}_logits_read", 1)
                self.router_max = Signal(f"{tag}_router_max", 1)
                self.router_exp = Signal(f"{tag}_router_exp", 1)
                self.top_diff = Signal(f"{tag}_top_diff", 1)
                self.top_exp = Signal(f"{tag}_top_exp", 1)
                self.h_psum = Signal(f"{tag}_h_psum", self.steps)
                self.th_ready = Signal(f"{tag}_th_ready", self.steps)
                self.gated_ready = Signal(f"{tag}_gated_ready", self.steps)
                self.hid_ready = Signal(f"{tag}_hid_ready", self.steps)
                self.y_psum = Signal(f"{tag}_y_psum", experts)
                self.y_added = Signal(f"{tag}_y_added", experts, before=1)

        mixtures = [
            Mixture("m0", E0 + 1, 1, lambda s: C_F1 + s * D, lambda s: C_F3 + s * D, lambda s: C_F2 + s * D,
                    C_FR, True, 1),
            Mixture("m1", E1, J1, lambda s: C_L1 + (s // J1 * 4 + J1 + s % J1) * D,
                    lambda s: C_L1 + (s // J1 * 4 + s % J1) * D, lambda s: C_L2 + s * D, C_LR, False, 3)]
        m0, m1 = mixtures

        def up_banks(s):
            return SHARED if s % 2 else B_TWO


        def run(order, i, steps):
            for offset, name, args in order:
                if name in steps:
                    steps[name](i + offset, *args)

        def passes(engine, steps):
            run(FIRST, 0, steps)
            with engine.Fori(0, UNITS - 2) as i:
                run(PASS, i, steps)
            run(LAST_BUT_ONE, UNITS - 2, steps)
            run(LAST, UNITS - 1, steps)

        block = ctx.enter_context(nc.Block())

        @block.sync
        def _(sp):
            sp.dma_start(VEC[:, 0:V_BV], vec[:, 0:V_BV]).then_inc(setup_dma[-1], 16)
            sp.dma_start(VEC[:, V_BV:C_VEC], vec[:, V_BV:C_VEC]).then_inc(x_stored.sem, 16)
            for b in range(2):
                sp.dma_start(xin[:, 2 * b:2 * b + 2, :], x_u[0][:, 2 * b:2 * b + 2, :]).then_inc(x_loaded.sem, 16)
            for k, (a, b, _) in enumerate(GROUPS):
                sp.dma_start(stage[:, a:b], wr[:, a:b]).then_inc(setup_dma[k], 16)
            sp.dma_start(WF[:, :], wf).then_inc(setup_dma[-2], 16)

            def load(i):
                for b in range(2):
                    sp.wait_ge(x_added.sem, x_added.at(i - 1, b + 1))
                    sp.dma_start(xin[:, 2 * b:2 * b + 2, :], x_u[i][:, 2 * b:2 * b + 2, :]).then_inc(x_loaded.sem, 16)

            def store(i):
                sp.wait_ge(m1.y_added.sem, m1.y_added.at(i, m1.experts))
                sp.dma_start(out_u[i], xr[:, :, :]).then_inc(x_stored.sem, 16)

            load(1)
            with sp.Fori(0, UNITS - 2) as i:
                load(i + 2)
                store(i)
            store(UNITS - 2)
            store(UNITS - 1)
            sp.wait_ge(x_stored.sem, x_stored.at(UNITS, 0))

        @block.gpsimd
        def _(pool):
            pool.memset(ident[:, :], 0.0).then_inc(ident_zero, 1)
            pool.wait_ge(ident_zero, 1)
            pool.affine_select(out=ident[:, :], in_=ident[:, :], compare_op=ALU.not_equal, fill=1.0, base=0,
                               pattern=[[-1, P]], channel_multiplier=1).then_inc(ident_ready, 1)
            pool.wait_ge(consts_ready, 1)
            pool.wait_ge(x_stored.sem, 16)

            def a_norm(i, b):
                pool.wait_ge(a_pow_arg.sem, a_pow_arg.at(i, b + 1))
                pool.tensor_tensor(prs_a[:, :], parg_a[:, :], half_neg[:, 0:2], ALU.pow).then_inc(a_pow_done.sem, 1)

            def head_norms(i, b, part, t):
                pool.wait_ge(ss_ready.sem, ss_ready.at(i, 4 * b + 2 * part + t + 1))
                heads = slice(part * H, part * H + H)
                pool.tensor_tensor(rn[:, t, heads], ss[:, t, heads], half_neg[:, 0:H], ALU.pow).then_inc(rn_ready.sem, 1)

            def power(i, k):
                rows = 2 if k == 0 else 1
                pool.wait_ge(b_pow_arg.sem, b_pow_arg.at(i, k + 1))
                pool.tensor_tensor(prs[:, 0:rows, :].rearrange("p a t -> p (a t)"),
                                   parg[:, 0:rows, :].rearrange("p a t -> p (a t)"),
                                   half_neg[:, 0:rows * T], ALU.pow).then_inc(b_pow_done.sem, 1)

            def l_turn_x(i):
                pool.wait_ge(b_xn.sem, b_xn.at(i, 3))
                bo = VEC[:, V_BO:V_BO + D].unsqueeze(1).broadcast_to([P, T, D])
                pool.tensor_tensor(xl[:, :, :], xr[:, :, :], bo, ALU.add).then_inc(l_xb.sem, 1)

            passes(pool, {
                "a_norm": a_norm, "a_qk": head_norms, "l_turn_x": l_turn_x, "b_norm": lambda i: power(i, 0),
                "f_norm": lambda i: power(i, 1), "l_norm": lambda i: power(i, 2), "l_norm2": lambda i: power(i, 3)})

        @block.tensor
        def _(pe):
            def split_mm(dst, lh, ll, rh, rl):
                pe.matmul(dst, lh, rh, start=True, stop=False)
                pe.matmul(dst, lh, rl, start=False, stop=False)
                return pe.matmul(dst, ll, rh, start=False, stop=True)

            def a_turn(i, b):
                pe.wait_ge(a_xn.sem, a_xn.at(i, b + 1))
                for t in range(2):
                    last = pe.transpose(bank(A_OUT)[:, t * P:t * P + P], xn_a[:, t, :], ident[:, :])
                last.then_inc(a_xT_psum.sem, 1)

            def a_rows(t, col):
                c = slice(t * P, t * P + P)
                for q in range(2):
                    w = slice(col + 512 * q, col + 512 * q + 512)
                    last = split_mm(bank(q), xTh_a[:, c], xTl_a[:, c], WH[:, w], WL[:, w])
                return last

            def a_qk(i, b, part, t):
                if part or t:
                    pe.wait_ge(raw_copied.sem, raw_copied.at(i, 4 * b + 2 * part + t))
                else:
                    pe.wait_ge(a_xT.sem, a_xT.at(i, b + 1))
                a_rows(t, C_QK + part * INNER).then_inc(qk_psum.sem, 1)

            def a_v(i, t):
                if t % 2:
                    pe.wait_ge(v_copied.sem, v_copied.at(i, t))
                else:
                    pe.wait_ge(raw_copied.sem, raw_copied.at(i, 2 * t + 4))
                a_rows(t % 2, C_V).then_inc(v_psum.sem, 1)

            def a_pairs(i, b, part, half):
                if part == 0 and half == 0:
                    pe.wait_ge(v_copied.sem, v_copied.at(i, 2 * b + 2))
                    pe.wait_ge(qk_normed.sem, qk_normed.at(i, 4 * b + 2))
                elif part == 0:
                    pe.wait_ge(qT_ready.sem, qT_ready.at(i, 2 * b + 1))
                elif half == 0:
                    pe.wait_ge(qT_ready.sem, qT_ready.at(i, 2 * b + 2))
                    pe.wait_ge(qk_normed.sem, qk_normed.at(i, 4 * b + 4))
                else:
                    pe.wait_ge(kT_ready.sem, kT_ready.at(i, 2 * b + 1))
                for n in range(HALF):
                    col = part * INNER + (half * HALF + n) * P
                    for t in range(2):
                        c0 = n % 2 * SEQ + t * P
                        last = pe.transpose(bank(n // 2)[:, c0:c0 + P], raw[:, t, col:col + P], ident[:, :])
                last.then_inc(pairs_psum.sem, 1)

            def a_scores(i, g):
                b, j, s = g // HP, g % HP, g % 2
                if j < 2:
                    pe.wait_ge(qT_ready.sem, qT_ready.at(i, 2 * b + 2))
                    pe.wait_ge(kT_ready.sem, kT_ready.at(i, 2 * b + 2))
                else:
                    pe.wait_ge(tanh_done.sem, tanh_done.at(i, g - 1))
                for kc in range(2):
                    for e in range(2):
                        rows = slice(e * DH, e * DH + DH)
                        last = pe.matmul(bank(2 * s + e)[:, kc * SEQ:kc * SEQ + SEQ], kT[rows, j, kc * P:kc * P + P],
                                         qT[rows, j, :], start=True, stop=True)
                last.then_inc(s_psum.sem, 1)

            def a_values(i, g):
                b, j = g // HP, g % HP
                pe.wait_ge(p_ready.sem, p_ready.at(i, g + 1))
                if j:
                    pe.wait_ge(o_normed.sem, o_normed.at(i, g))
                for qc in range(2):
                    for e in range(2):
                        c0 = (qc * 2 + e) * (DH + 1)
                        for kc in range(2):
                            last = pe.matmul(bank(A_OUT)[:, c0:c0 + DH + 1], pT[:, g % 3, e, kc, qc * P:qc * P + P],
                                             vx[:, kc, 2 * j + e, :], start=(kc == 0), stop=(kc == 1))
                last.then_inc(o_psum.sem, 1)

            def a_turn_out(i, t):
                b = t // 2
                if t % 2 == 0:
                    pe.wait_ge(o_normed.sem, o_normed.at(i, HP * (b + 1)))
                    pe.wait_ge(tanh_done.sem, tanh_done.at(i, HP * (b + 1)))
                for j in range(HP):
                    last = pe.transpose(bank(t % 2 * 2 + j // 4)[:, j % 4 * P:j % 4 * P + P],
                                        ao[:, t % 2, j * P:j * P + P], ident[:, :])
                last.then_inc(aoT_psum.sem, 1)

            def a_out(i, b):
                for t in (2 * b, 2 * b + 1):
                    pe.wait_ge(aoT_act.sem, aoT_act.at(i, t + 1))
                    pe.wait_ge(aoT_dve.sem, aoT_dve.at(i, t + 1))
                    for j in range(HP):
                        last = pe.matmul(bank(A_OUT)[:, t % 2 * D:t % 2 * D + D], aoT[:, t % 2, j * P:j * P + P],
                                         WF[:, C_WO + j * D:C_WO + j * D + D], start=(j == 0), stop=(j == HP - 1))
                last.then_inc(wo_psum.sem, 1)

            def w_T(dst, col):
                return split_mm(dst, WH[:, col:col + P], WL[:, col:col + P], xTh[:, :], xTl[:, :])

            def w_rows(dst, t, col, n):
                c = slice(t * P, t * P + P)
                return split_mm(dst, xTh[:, c], xTl[:, c], WH[:, col:col + n], WL[:, col:col + n])

            def turn_x(i, k):
                pe.wait_ge(b_xn.sem, b_xn.at(i, k + 1))
                if k == 0:
                    pe.wait_ge(m1.y_added.sem, m1.y_added.at(i, 0))
                for t in range(T):
                    last = pe.transpose(bank(B_ONE)[:, t * P:t * P + P], xn[:, t, :], ident[:, :])
                last.then_inc(b_xT_psum.sem, 1)

            def f_project(i):
                pe.wait_ge(b_xT.sem, b_xT.at(i, 1))
                w_T(bank(B_TWO), C_FQ).then_inc(f_proj.sem, 1)
                w_T(bank(B_TWO + 1), C_FK).then_inc(f_proj.sem, 1)
                for t in range(T):
                    last = w_rows(bank(B_ONE)[:, t * FD:t * FD + FD], t, C_FV, FD)
                last.then_inc(f_proj.sem, 1)

            def f_scores(i, t):
                if t == 0:
                    pe.wait_ge(fq_ready.sem, fq_ready.at(i, 1))
                    pe.wait_ge(fk_ready.sem, fk_ready.at(i, 1))
                else:
                    pe.wait_ge(f_pT_act.sem, f_pT_act.at(i, t))
                    pe.wait_ge(f_pT_dve.sem, f_pT_dve.at(i, t))
                k0 = t // 2 * SEQ
                for h in range(FH):
                    last = pe.matmul(bank(B_TWO + h // 2)[:, h % 2 * SEQ:h % 2 * SEQ + SEQ], fqz[:, h, t * P:t * P + P],
                                     fk[:, k0:k0 + SEQ], start=True, stop=True)
                last.then_inc(f_scores_psum.sem, 1)

            def f_turn(i, t):
                pe.wait_ge(f_p.sem, f_p.at(i, t + 1))
                for m in range(2 * FH):
                    last = pe.transpose(bank(B_TWO + m // 4)[:, m % 4 * P:m % 4 * P + P],
                                        fp[:, m // 2, m % 2 * P:m % 2 * P + P], ident[:, :])
                last.then_inc(f_pT_psum.sem, 1)

            def f_values(i, t):
                pe.wait_ge(f_pT_act.sem, f_pT_act.at(i, t + 1))
                pe.wait_ge(f_pT_dve.sem, f_pT_dve.at(i, t + 1))
                if t == 0:
                    pe.wait_ge(fv_ready.sem, fv_ready.at(i, 1))
                else:
                    pe.wait_ge(f_o.sem, f_o.at(i, t))
                for h in range(FH):
                    for kc in range(2):
                        last = pe.matmul(bank(B_ONE)[:, h * (FD + 1):(h + 1) * (FD + 1)], fpT[:, 2 * h + kc, :],
                                         fv[:, t // 2 * 2 + kc, :], start=(kc == 0), stop=(kc == 1))
                last.then_inc(f_o_psum.sem, 1)

            def f_turn_out(i):
                pe.wait_ge(f_o.sem, f_o.at(i, T))
                for t in range(T):
                    last = pe.transpose(bank(B_TWO)[:, t * P:t * P + P], fo[:, t, :], ident[:, :])
                last.then_inc(f_oT_psum.sem, 1)

            def f_out(i):
                pe.wait_ge(f_oT.sem, f_oT.at(i, 1))
                for t in range(T):
                    last = pe.matmul(bank(B_TWO + 1)[:, t * P:t * P + P], foT[:, t * P:t * P + P],
                                     WF[:, C_FWO:C_FWO + D], start=True, stop=True)
                last.then_inc(f_wo.sem, 1)

            def l_project(i):
                pe.wait_ge(b_xT.sem, b_xT.at(i, 3))
                w_T(bank(B_TWO), C_LQ).then_inc(l_proj.sem, 1)
                w_T(bank(B_TWO + 1), C_LK).then_inc(l_proj.sem, 1)
                for t in range(T):
                    last = w_rows(bank(B_ONE)[:, t * P:t * P + P], t, C_LV, D)
                last.then_inc(l_proj.sem, 1)

            def l_scores(i):
                pe.wait_ge(lqk_ready.sem, lqk_ready.at(i, 2))
                for b in range(2):
                    for qc in range(2):
                        t = 2 * b + qc
                        last = pe.matmul(bank(B_TWO + b)[:, qc * SEQ:qc * SEQ + SEQ], lq[:, t * P:t * P + P],
                                         lk[:, b * SEQ:b * SEQ + SEQ], start=True, stop=True)
                    last.then_inc(l_scores_psum.sem, 1)

            def l_turn(i):
                for b in range(2):
                    pe.wait_ge(l_p.sem, l_p.at(i, b + 1))
                    for m in range(4):
                        qc, kc = m // 2, m % 2
                        last = pe.transpose(bank(B_TWO + b)[:, m * P:m * P + P], lp[:, 2 * b + qc, kc * P:kc * P + P],
                                            ident[:, :])
                    last.then_inc(l_pT_psum.sem, 1)

            def l_values(i):
                pe.wait_ge(lv_ready.sem, lv_ready.at(i, 1))
                for b in range(2):
                    if b == 0:
                        pe.wait_ge(l_pT_dve.sem, l_pT_dve.at(i, 1))
                    else:
                        pe.wait_ge(l_pT_act.sem, l_pT_act.at(i, 1))
                    for qc in range(2):
                        for kc in range(2):
                            last = pe.matmul(bank(B_ONE + b)[:, qc * (D + 1):(qc + 1) * (D + 1)],
                                             lpT[:, b, 2 * qc + kc, :], lv[:, 2 * b + kc, :], start=(kc == 0), stop=(kc == 1))
                    last.then_inc(l_o_psum.sem, 1)

            def l_turn_out(i):
                pe.wait_ge(l_o.sem, l_o.at(i, 2))
                for t in range(T):
                    last = pe.transpose(bank(B_TWO + 1)[:, t * P:t * P + P], lo[:, t, :], ident[:, :])
                last.then_inc(l_oT_psum.sem, 1)

            def l_out(i):
                pe.wait_ge(l_oT.sem, l_oT.at(i, 1))
                for t in range(T):
                    last = pe.matmul(bank(B_ONE)[:, t * P:t * P + P], loT[:, t * P:t * P + P], WF[:, C_LWO:C_LWO + D],
                                     start=True, stop=True)
                last.then_inc(l_wo.sem, 1)

            def m_router(i, k):
                m = mixtures[k]
                pe.wait_ge(b_xT.sem, b_xT.at(i, m.norm + 1))
                for t in range(T):
                    last = w_rows(bank(B_ONE)[:, t * 8:t * 8 + 8], t, m.router_col, 8)
                last.then_inc(m.router_psum.sem, 1)

            def m_up(i, k, s):
                m = mixtures[k]
                if s >= 2:
                    pe.wait_ge(m.hid_ready.sem, m.hid_ready.at(i, s - 1))
                w_T(bank(up_banks(s)), m.gate_col(s))
                w_T(bank(up_banks(s) + 1), m.value_col(s)).then_inc(m.h_psum.sem, 1)

            def m_down(i, k, e):
                m = mixtures[k]
                pe.wait_ge(m.hid_ready.sem, m.hid_ready.at(i, (e + 1) * m.parts))
                if e:
                    pe.wait_ge(m.y_added.sem, m.y_added.at(i, e))
                else:
                    pe.wait_ge(m.logits_read.sem, m.logits_read.at(i, 1))
                for t in range(T):
                    for j in range(m.parts):
                        s = e * m.parts + j
                        last = pe.matmul(bank(B_ONE)[:, t * P:t * P + P], hid[:, s % 4, t * P:t * P + P],
                                         WF[:, m.down_col(s):m.down_col(s) + D], start=(j == 0), stop=(j == m.parts - 1))
                last.then_inc(m.y_psum.sem, 1)

            pe.wait_ge(ident_ready, 1)
            pe.wait_ge(weights_ready, 1)
            pe.wait_ge(setup_dma[-2], 16)
            passes(pe, {
                "a_turn": a_turn, "a_qk": a_qk, "a_v": a_v, "a_pairs": a_pairs, "a_scores": a_scores,
                "a_values": a_values, "a_turn_out": a_turn_out, "a_out": a_out,
                "f_turn_x": lambda i: turn_x(i, 0), "f_project": f_project, "f_scores": f_scores, "f_turn": f_turn,
                "f_values": f_values, "f_turn_out": f_turn_out, "f_out": f_out,
                "l_turn_x": lambda i: turn_x(i, 2), "l_project": l_project, "l_scores": l_scores, "l_turn": l_turn,
                "l_values": l_values, "l_turn_out": l_turn_out, "l_out": l_out,
                "m_turn_x": lambda i, k: turn_x(i, mixtures[k].norm), "m_router": m_router, "m_up": m_up,
                "m_down": m_down})

        @block.scalar
        def _(act):
            def a_qk(i, b, part, t):
                q = 4 * b + 2 * part + t
                features = raw[:, t, part * INNER:part * INNER + INNER]
                act.wait_ge(qk_psum.sem, qk_psum.at(i, q + 1))
                act.activation(features, banks(0, 2), ACT.Copy).then_inc(raw_copied.sem, 1)
                act.wait_ge(raw_copied.sem, raw_copied.at(i, q + 1))
                if q % 4 >= 2:
                    act.wait_ge(ss_ready.sem, ss_ready.at(i, q - 1))
                act.activation(sq[:, t, :], features, ACT.Square).then_inc(squared.sem, 1)

            def a_v(i, t):
                act.wait_ge(v_psum.sem, v_psum.at(i, t + 1))
                act.activation(vx[:, t % 2, :, 0:DH], banks(0, 2).rearrange("p (h d) -> p h d", h=H), ACT.Copy)\
                   .then_inc(v_copied.sem, 1)

            def a_pairs(i, b, part, half):
                if part == 0:
                    act.wait_ge(pairs_psum.sem, pairs_psum.at(i, 4 * b + half + 1))
                    act.activation(qT[:, half * HALF:(half + 1) * HALF, :].rearrange("p j n -> p (j n)"), banks(0, 2),
                                   ACT.Copy).then_inc(qT_ready.sem, 1)

            def exponent(i, g):
                act.wait_ge(tanh_done.sem, tanh_done.at(i, g + 1))
                v = pT[:, g % 3].rearrange("p a b c -> p (a b c)")
                act.activation(v, v, ACT.Exp, scale=CLAMP * DH ** -0.5).then_inc(p_ready.sem, 1)

            def a_scores(i, g):
                act.wait_ge(s_psum.sem, s_psum.at(i, g + 1))
                if g % HP == 0:
                    act.wait_ge(ss_ready.sem, ss_ready.at(i, 4 * (g // HP) + 4))
                if g % HP >= 3:
                    act.wait_ge(o_psum.sem, o_psum.at(i, g - 2))
                act.activation(pT[:, g % 3].rearrange("p a b c -> p (a b c)"), banks(2 * (g % 2), 2), ACT.Tanh,
                               scale=DH / CLAMP).then_inc(tanh_done.sem, 1)
                if g % HP:
                    exponent(i, g - 1)

            def a_values(i, g):
                if g % HP == HP - 2:
                    exponent(i, g + 1)

            def a_turn_out(i, t):
                act.wait_ge(aoT_psum.sem, aoT_psum.at(i, t + 1))
                act.activation(aoT[:, t % 2, 0:512], bank(t % 2 * 2), ACT.Copy).then_inc(aoT_act.sem, 1)

            def f_project(i):
                act.wait_ge(f_proj.sem, f_proj.at(i, 1))
                for h in range(FH):
                    rows = slice(h * FD, h * FD + FD)
                    last = act.activation(fqz[rows, h, :], bank(B_TWO)[rows, :], ACT.Copy, scale=FD ** -0.5)
                last.then_inc(fq_ready.sem, 1)

            def f_scores(i, t):
                act.wait_ge(f_max.sem, f_max.at(i, t + 1))
                for h in range(FH):
                    last = act.activation(fp[:, h, :], bank(B_TWO + h // 2)[:, h % 2 * SEQ:h % 2 * SEQ + SEQ], ACT.Exp,
                                          bias=nm[:, t % 2, h:h + 1])
                last.then_inc(f_p.sem, 1)

            def f_turn(i, t):
                act.wait_ge(f_pT_psum.sem, f_pT_psum.at(i, t + 1))
                act.activation(fpT[:, 0:4, :].rearrange("p m q -> p (m q)"), bank(B_TWO), ACT.Copy)\
                   .then_inc(f_pT_act.sem, 1)

            def f_turn_out(i):
                act.wait_ge(f_oT_psum.sem, f_oT_psum.at(i, 1))
                act.activation(foT, bank(B_TWO), ACT.Copy).then_inc(f_oT.sem, 1)

            def f_norm(i):
                act.wait_ge(x2_ready.sem, x2_ready.at(i, 1))
                for t in range(T):
                    last = act.activation(xn[:, t, :], xl[:, t, :], ACT.Square, accum_out=ms[:, t:t + 1])
                last.then_inc(x2_squares.sem, 1)

            def l_project(i):
                act.wait_ge(l_proj.sem, l_proj.at(i, 1))
                act.activation(lq, bank(B_TWO), ACT.Identity, bias=VEC[:, V_BQ:V_BQ + 1]).then_inc(lqk_ready.sem, 1)
                act.wait_ge(l_proj.sem, l_proj.at(i, 2))
                act.activation(lk, bank(B_TWO + 1), ACT.Identity, bias=VEC[:, V_BK:V_BK + 1]).then_inc(lqk_ready.sem, 1)

            def l_scores(i):
                for b in range(2):
                    act.wait_ge(l_scores_psum.sem, l_scores_psum.at(i, b + 1))
                    act.activation(ltheta[:, b, :], bank(B_TWO + b), ACT.Relu)
                    if b:
                        act.wait_ge(l_theta.sem, l_theta.at(i, 1))
                    act.activation(lth, bank(B_TWO + b), ACT.Tanh, scale=0.5)
                    act.activation(lth2, bank(B_TWO + b), ACT.Tanh).then_inc(l_maps.sem, 1)
                for b in range(2):
                    act.wait_ge(l_max.sem, l_max.at(i, b + 1))
                    for qc in range(2):
                        last = act.activation(lp[:, 2 * b + qc, :], ltheta[:, b, qc * SEQ:qc * SEQ + SEQ], ACT.Exp,
                                              scale=0.1, bias=nm[:, b, 2 + qc:3 + qc])
                    last.then_inc(l_p.sem, 1)

            def l_turn(i):
                act.wait_ge(l_pT_psum.sem, l_pT_psum.at(i, 2))
                act.activation(lpT[:, 1].rearrange("p m q -> p (m q)"), bank(B_TWO + 1), ACT.Copy).then_inc(l_pT_act.sem, 1)

            def l_turn_out(i):
                act.wait_ge(l_oT_psum.sem, l_oT_psum.at(i, 1))
                act.activation(loT, bank(B_TWO + 1), ACT.Copy).then_inc(l_oT.sem, 1)

            def m_top_a(i, k):
                m = mixtures[k]
                if m.shared:
                    act.wait_ge(m.router_max.sem, m.router_max.at(i, 1))
                    act.activation(small[:, 1, :], small[:, 0, :], ACT.Exp).then_inc(m.router_exp.sem, 1)

            def m_top_b(i, k):
                m = mixtures[k]
                act.wait_ge(m.top_diff.sem, m.top_diff.at(i, 1))
                act.activation(small[:, 5, 0:T], small[:, 4, 0:T], ACT.Exp).then_inc(m.top_exp.sem, 1)

            def m_up(i, k, s):
                m = mixtures[k]
                act.wait_ge(m.h_psum.sem, m.h_psum.at(i, s + 1))
                if s >= 2:
                    act.wait_ge(m.gated_ready.sem, m.gated_ready.at(i, s - 1))
                act.activation(th[:, s % 2, :], bank(up_banks(s)), ACT.Tanh, scale=0.5).then_inc(m.th_ready.sem, 1)

            act.wait_ge(setup_dma[-1], 16)
            act.wait_ge(fqz_zero, 1)
            passes(act, {
                "a_qk": a_qk, "a_v": a_v, "a_pairs": a_pairs, "a_scores": a_scores, "a_values": a_values,
                "a_turn_out": a_turn_out, "f_project": f_project, "f_scores": f_scores, "f_turn": f_turn,
                "f_turn_out": f_turn_out, "f_norm": f_norm, "l_project": l_project, "l_scores": l_scores,
                "l_turn": l_turn, "l_turn_out": l_turn_out, "m_top_a": m_top_a, "m_top_b": m_top_b, "m_up": m_up})

        @block.vector
        def _(dve):
            def link(chain, i, ins):
                chain.links = chain.links % chain.per_unit + 1
                ins.then_inc(chain.sem, 1)
                dve.wait_ge(chain.sem, chain.at(i, chain.links))

            def moments(chain, i, dst, st, src, n, touch):
                for t in range(n):
                    last = dve.bn_stats(st[:, t, :], src[:, t, :])
                link(chain, i, last)
                dve.tensor_copy(touch[:, 1:2], touch[:, 0:1])
                for t in range(n):
                    last = dve.bn_aggr(dst[:, t, :], st[:, t, :])
                link(chain, i, last)

            def a_norm(i, b):
                dve.wait_ge(x_loaded.sem, x_loaded.at(i, 16 * (b + 1)))
                src = xin[:, 2 * b:2 * b + 2, :]
                moments(chain_x, i, mv_a, stats_a, src, 2, touch_a)
                dve.tensor_scalar(parg_a[:, :], mv_a[:, :, 1], 1.0 + RMS0_EPS, RMS0_EPS * LN_EPS, ALU.mult, ALU.add)\
                   .then_inc(a_pow_arg.sem, 1)

            def a_turn(i, b):
                src = xin[:, 2 * b:2 * b + 2, :]
                dve.wait_ge(a_pow_done.sem, a_pow_done.at(i, b + 1))
                for t in range(2):
                    last = dve.tensor_scalar(xn_a[:, t, :], src[:, t, :], mv_a[:, t, 0:1], prs_a[:, t:t + 1],
                                             ALU.subtract, ALU.mult)
                last.then_inc(a_xn.sem, 1)
                dve.wait_ge(a_xT_psum.sem, a_xT_psum.at(i, b + 1))
                link(chain_x, i, dve.tensor_copy(xTh_a[:, :], bank(A_OUT, SEQ)))
                dve.tensor_tensor(xTl_a[:, :], bank(A_OUT, SEQ), xTh_a[:, :].bitcast(F32), ALU.subtract).then_inc(a_xT.sem, 1)

            def a_qk(i, b, part, t):
                q = 4 * b + 2 * part + t
                sums = ss[:, t, part * H:part * H + H]
                dve.wait_ge(squared.sem, squared.at(i, q + 1))
                link(chain_a, i, dve.tensor_reduce(sums, sq[:, t, :].rearrange("p (h d) -> p h d", d=DH), AX_X, ALU.add))
                dve.tensor_scalar(sums, sums, 1e-24, None, ALU.max).then_inc(ss_ready.sem, 1)

            def a_scale(i, b, part, t):
                dve.wait_ge(rn_ready.sem, rn_ready.at(i, 4 * b + 2 * part + t + 1))
                v = raw[:, t, part * INNER:part * INNER + INNER].rearrange("p (h d) -> p h d", d=DH)
                dve.tensor_tensor(v, v, rn[:, t, part * H:part * H + H].unsqueeze(2).broadcast_to([P, H, DH]), ALU.mult)\
                   .then_inc(qk_normed.sem, 1)

            def a_pairs(i, b, part, half):
                if part == 1:
                    js = slice(half * HALF, (half + 1) * HALF)
                    dve.wait_ge(pairs_psum.sem, pairs_psum.at(i, 4 * b + 2 + half + 1))
                    dve.tensor_tensor(kT[:, js, :], banks(0, 2).rearrange("p (j n) -> p j n", j=HALF),
                                      gamma[:, js].unsqueeze(2).broadcast_to([P, HALF, SEQ]), ALU.mult)\
                       .then_inc(kT_ready.sem, 1)

            def a_values(i, g):
                j = g % HP
                o = bank(A_OUT, 4 * (DH + 1)).rearrange("p (m d) -> p m d", d=DH + 1)
                dve.wait_ge(o_psum.sem, o_psum.at(i, g + 1))
                link(chain_a, i, dve.reciprocal(rd_a[:, g % 2, :], o[:, :, DH]))
                dve.tensor_tensor(ao[:, :, j * P:j * P + P].rearrange("p q (e d) -> p q e d", e=2),
                                  o[:, :, 0:DH].rearrange("p (q e) d -> p q e d", e=2),
                                  rd_a[:, g % 2, :].rearrange("p (q e) -> p q e", e=2).unsqueeze(3).broadcast_to([P, 2, 2, DH]),
                                  ALU.mult).then_inc(o_normed.sem, 1)

            def a_turn_out(i, t):
                dve.wait_ge(aoT_psum.sem, aoT_psum.at(i, t + 1))
                dve.tensor_copy(aoT[:, t % 2, 512:1024], bank(t % 2 * 2 + 1)).then_inc(aoT_dve.sem, 1)

            def a_out(i, b):
                dve.wait_ge(wo_psum.sem, wo_psum.at(i, b + 1))
                if b == 0:
                    dve.wait_ge(x2_ready.sem, x2_ready.at(i, 0))
                dve.tensor_tensor(xa[:, 2 * b:2 * b + 2, :], xin[:, 2 * b:2 * b + 2, :],
                                  bank(A_OUT, SEQ).rearrange("p (t d) -> p t d", t=2), ALU.add).then_inc(x_added.sem, 1)

            def centre(dst, src, row):
                for t in range(T):
                    last = dve.tensor_scalar(dst[:, t, :], src[:, t, :], mv[:, t, 0:1], prs[:, row, t:t + 1],
                                             ALU.subtract, ALU.mult)
                return last

            def split_xT(i, k):
                dve.wait_ge(b_xT_psum.sem, b_xT_psum.at(i, k + 1))
                link(chain_b, i, dve.tensor_copy(xTh[:, :], bank(B_ONE)))
                dve.tensor_tensor(xTl[:, :], bank(B_ONE), xTh[:, :].bitcast(F32), ALU.subtract).then_inc(b_xT.sem, 1)

            def b_norm(i):
                dve.wait_ge(x_added.sem, x_added.at(i, 2))
                moments(chain_n, i, mv, stats, xa, T, touch_b)
                dve.tensor_scalar(parg[:, 0, :], mv[:, :, 1], 1.0 + RMS1_EPS, RMS1_EPS * LN_EPS, ALU.mult, ALU.add)
                dve.tensor_scalar(parg[:, 1, :], mv[:, :, 1], LN_EPS, None, ALU.add).then_inc(b_pow_arg.sem, 1)
                dve.wait_ge(b_pow_done.sem, b_pow_done.at(i, 1))
                centre(xn, xa, 0).then_inc(b_xn.sem, 1)
                centre(xl, xa, 1)

            def f_project(i):
                dve.wait_ge(f_proj.sem, f_proj.at(i, 2))
                dve.tensor_copy(fk, bank(B_TWO + 1)).then_inc(fk_ready.sem, 1)
                dve.wait_ge(f_proj.sem, f_proj.at(i, 3))
                dve.tensor_copy(fv[:, :, 0:FD], bank(B_ONE, T * FD).rearrange("p (t d) -> p t d", t=T))\
                   .then_inc(fv_ready.sem, 1)

            def f_scores(i, t):
                dve.wait_ge(f_scores_psum.sem, f_scores_psum.at(i, t + 1))
                dve.tensor_reduce(nm[:, t % 2, :], banks(B_TWO, 2).rearrange("p (h k) -> p h k", h=FH),
                                  AX_X, ALU.max, negate=True).then_inc(f_max.sem, 1)

            def f_turn(i, t):
                dve.wait_ge(f_pT_psum.sem, f_pT_psum.at(i, t + 1))
                dve.tensor_copy(fpT[:, 4:8, :].rearrange("p m q -> p (m q)"), bank(B_TWO + 1)).then_inc(f_pT_dve.sem, 1)

            def f_values(i, t):
                o = bank(B_ONE, FH * (FD + 1)).rearrange("p (h d) -> p h d", h=FH)
                dve.wait_ge(f_o_psum.sem, f_o_psum.at(i, t + 1))
                link(chain_b, i, dve.reciprocal(rd[:, :], o[:, :, FD]))
                dve.tensor_tensor(fo[:, t, :].rearrange("p (h d) -> p h d", h=FH), o[:, :, 0:FD],
                                  rd[:, :].unsqueeze(2).broadcast_to([P, FH, FD]), ALU.mult).then_inc(f_o.sem, 1)

            def f_out(i):
                dve.wait_ge(f_wo.sem, f_wo.at(i, 1))
                dve.wait_ge(x_stored.sem, x_stored.at(i, 0))
                rows = bank(B_TWO + 1).rearrange("p (t d) -> p t d", t=T)
                link(chain_b, i, dve.tensor_tensor(xl[:, :, :], xl[:, :, :], rows, ALU.add))
                dve.tensor_tensor(xr[:, :, :], xa[:, :, :], xl[:, :, :], ALU.add).then_inc(x2_ready.sem, 1)

            def f_norm(i):
                dve.wait_ge(x2_squares.sem, x2_squares.at(i, 1))
                dve.tensor_scalar(parg[:, 0, :], ms[:, :], 1.0 / D, RMS1_EPS, ALU.mult, ALU.add).then_inc(b_pow_arg.sem, 1)
                dve.wait_ge(b_pow_done.sem, b_pow_done.at(i, 2))
                for t in range(T):
                    last = dve.tensor_scalar(xn[:, t, :], xl[:, t, :], prs[:, 0, t:t + 1], None, ALU.mult)
                last.then_inc(b_xn.sem, 1)

            def norm_xr(i, k):
                moments(chain_b, i, mv, stats, xr, T, touch_b)
                dve.tensor_scalar(parg[:, 0, :], mv[:, :, 1], LN_EPS, None, ALU.add).then_inc(b_pow_arg.sem, 1)
                dve.wait_ge(b_pow_done.sem, b_pow_done.at(i, k + 1))
                centre(xn, xr, 0).then_inc(b_xn.sem, 1)

            def l_norm(i):
                dve.wait_ge(m0.y_added.sem, m0.y_added.at(i, m0.experts))
                norm_xr(i, 2)

            def l_project(i):
                dve.wait_ge(l_proj.sem, l_proj.at(i, 3))
                bv = VEC[:, V_BV:V_BV + D].unsqueeze(1).broadcast_to([P, T, D])
                dve.tensor_tensor(lv[:, :, 0:D], bank(B_ONE).rearrange("p (t d) -> p t d", t=T), bv, ALU.add)\
                   .then_inc(lv_ready.sem, 1)

            def l_scores(i):
                for b in range(2):
                    dve.wait_ge(l_maps.sem, l_maps.at(i, b + 1))
                    link(chain_b, i, dve.scalar_tensor_tensor(ltheta[:, b, :], lth, 6.0, ltheta[:, b, :], ALU.add, ALU.add))
                    dve.scalar_tensor_tensor(ltheta[:, b, :], lth2, 1.5, ltheta[:, b, :], ALU.mult, ALU.add)\
                       .then_inc(l_theta.sem, 1)
                    dve.wait_ge(l_theta.sem, l_theta.at(i, b + 1))
                    link(chain_b, i, dve.tensor_reduce(nm[:, b, 0:2], ltheta[:, b, :].rearrange("p (q k) -> p q k", q=2),
                                                       AX_X, ALU.max, negate=True))
                    dve.tensor_scalar(nm[:, b, 2:4], nm[:, b, 0:2], 0.1, None, ALU.mult).then_inc(l_max.sem, 1)

            def l_turn(i):
                dve.wait_ge(l_pT_psum.sem, l_pT_psum.at(i, 1))
                dve.tensor_copy(lpT[:, 0].rearrange("p m q -> p (m q)"), bank(B_TWO)).then_inc(l_pT_dve.sem, 1)

            def l_values(i):
                for b in range(2):
                    o = bank(B_ONE + b, 2 * (D + 1)).rearrange("p (q d) -> p q d", q=2)
                    dve.wait_ge(l_o_psum.sem, l_o_psum.at(i, b + 1))
                    link(chain_b, i, dve.reciprocal(rd[:, 2 * b:2 * b + 2], o[:, :, D]))
                    dve.tensor_tensor(lo[:, 2 * b:2 * b + 2, :], o[:, :, 0:D],
                                      rd[:, 2 * b:2 * b + 2].unsqueeze(2).broadcast_to([P, 2, D]), ALU.mult)\
                       .then_inc(l_o.sem, 1)

            def l_out(i):
                dve.wait_ge(l_wo.sem, l_wo.at(i, 1))
                dve.wait_ge(l_xb.sem, l_xb.at(i, 1))
                dve.tensor_tensor(xr[:, :, :], xl[:, :, :], bank(B_ONE).rearrange("p (t d) -> p t d", t=T), ALU.add)\
                   .then_inc(l_x.sem, 1)

            def l_norm2(i):
                dve.wait_ge(l_x.sem, l_x.at(i, 1))
                norm_xr(i, 3)

            def experts_of(row):
                return small[:, row, :].rearrange("p (t e) -> p t e", t=T)

            def per_token(row):
                return small[:, row, 0:T].unsqueeze(2).broadcast_to([P, T, 8])

            def m_router(i, k):
                m = mixtures[k]
                logits = bank(B_ONE, T * 8)
                dve.wait_ge(m.router_psum.sem, m.router_psum.at(i, 1))
                if m.shared:
                    eb = VEC[:, V_EB:V_EB + 8].unsqueeze(1).broadcast_to([P, T, 8])
                    dve.tensor_tensor(experts_of(0), logits.rearrange("p (t e) -> p t e", t=T), eb, ALU.add)\
                       .then_inc(m.logits_read.sem, 1)
                    dve.wait_ge(m.logits_read.sem, m.logits_read.at(i, 1))
                    link(chain_b, i, dve.tensor_reduce(small[:, 6, 0:T], experts_of(0), AX_X, ALU.max))
                    dve.tensor_tensor(experts_of(0), experts_of(0), per_token(6), ALU.subtract).then_inc(m.router_max.sem, 1)
                else:
                    dve.tensor_copy(small[:, 2, :], logits).then_inc(m.logits_read.sem, 1)

            def m_top_a(i, k):
                m = mixtures[k]
                if m.shared:
                    dve.wait_ge(m.router_exp.sem, m.router_exp.at(i, 1))
                    link(chain_b, i, dve.tensor_reduce(small[:, 7, 0:T], experts_of(1), AX_X, ALU.add))
                    link(chain_b, i, dve.reciprocal(small[:, 8, 0:T], small[:, 7, 0:T]))
                    link(chain_b, i, dve.tensor_tensor(experts_of(2), experts_of(1), per_token(8), ALU.mult))
                else:
                    dve.wait_ge(m.logits_read.sem, m.logits_read.at(i, 1))
                dve.tensor_copy(touch_b[:, 1:2], touch_b[:, 0:1])
                for t in range(T):
                    last = dve.max(experts_of(3)[:, t, :], experts_of(2)[:, t, :])
                link(chain_b, i, last)
                dve.tensor_tensor(small[:, 4, 0:T], experts_of(3)[:, :, 1], experts_of(3)[:, :, 0], ALU.subtract)\
                   .then_inc(m.top_diff.sem, 1)
                for t in range(T):
                    last = dve.max_index(idx8[:, t, :], experts_of(3)[:, t, :], experts_of(2)[:, t, :])
                link(chain_b, i, last)
                link(chain_b, i, dve.tensor_copy(experts_of(9), idx8[:, :, :]))

            def m_top_b(i, k):
                lane = iota8[:, :].unsqueeze(1).broadcast_to([P, T, 8])
                for n in range(2):
                    last = dve.tensor_tensor(experts_of(10 + n), lane, experts_of(9)[:, :, n:n + 1].broadcast_to([P, T, 8]),
                                             ALU.is_equal)
                link(chain_b, i, last)

            def m_top_c(i, k):
                m = mixtures[k]
                dve.wait_ge(m.top_exp.sem, m.top_exp.at(i, 1))
                link(chain_b, i, dve.tensor_scalar(small[:, 6, 0:T], small[:, 5, 0:T], 2.0, 2.0, ALU.mult, ALU.add))
                link(chain_b, i, dve.reciprocal(small[:, 7, 0:T], small[:, 6, 0:T]))
                link(chain_b, i, dve.tensor_tensor(small[:, 8, 0:T], small[:, 7, 0:T], small[:, 5, 0:T], ALU.mult))
                for n in range(2):
                    last = dve.tensor_tensor(experts_of(10 + n), experts_of(10 + n), per_token(7 + n), ALU.mult)
                link(chain_b, i, last)
                link(chain_b, i, dve.tensor_tensor(comb[:, :, :], experts_of(10), experts_of(11), ALU.add))

            def m_up(i, k, s):
                m = mixtures[k]
                dve.wait_ge(m.th_ready.sem, m.th_ready.at(i, s + 1))
                dve.scalar_tensor_tensor(gated[:, s % 2, :], th[:, s % 2, :], 1.0, bank(up_banks(s)), ALU.add, ALU.mult)\
                   .then_inc(m.gated_ready.sem, 1)
                dve.wait_ge(m.gated_ready.sem, m.gated_ready.at(i, s + 1))
                if s >= 4:
                    dve.wait_ge(m.y_psum.sem, m.y_psum.at(i, (s - 4) // m.parts + 1))
                dve.tensor_tensor(hid[:, s % 4, :], gated[:, s % 2, :], bank(up_banks(s) + 1), ALU.mult)\
                   .then_inc(m.hid_ready.sem, 1)

            def m_down(i, k, e):
                m = mixtures[k]
                dve.wait_ge(m.y_psum.sem, m.y_psum.at(i, e + 1))
                if e:
                    dve.wait_ge(m.y_added.sem, m.y_added.at(i, e))
                y = bank(B_ONE)
                if m.shared and e == 0:
                    flat = xr[:, :, :].rearrange("p t d -> p (t d)")
                    last = dve.scalar_tensor_tensor(flat, y, 0.5, flat, ALU.mult, ALU.add)
                else:
                    c = e - 1 if m.shared else e
                    for t in range(T):
                        last = dve.scalar_tensor_tensor(xr[:, t, :], y[:, t * P:t * P + P], comb[:, t, c:c + 1],
                                                        xr[:, t, :], ALU.mult, ALU.add)
                last.then_inc(m.y_added.sem, 1)

            dve.memset(half_neg[:, :], -0.5).then_inc(consts_ready, 1)
            dve.memset(vx[:, :, :, DH:DH + 1], 1.0)
            dve.memset(fqz[:, :, :], 0.0).then_inc(fqz_zero, 1)
            dve.memset(fv[:, :, FD:FD + 1], 1.0)
            dve.memset(lv[:, :, D:D + 1], 1.0)
            dve.memset(touch_a[:, :], 1.0).then_inc(x2_ready.sem, 1)
            dve.memset(touch_b[:, :], 1.0).then_inc(m1.y_added.sem, 1)
            dve.memset(comb[:, :, :], 0.0).then_inc(m0.y_added.sem, 1)
            for e in range(8):
                dve.memset(iota8[:, e:e + 1], float(e))
            dve.wait_ge(setup_dma[-1], 16)
            dve.tensor_scalar(gamma[:, :], VEC[:, V_KG:V_KG + HP], 1.0, None, ALU.add).then_inc(consts_ready, 1)
            dve.wait_ge(consts_ready, 2)
            dve.scalar_tensor_tensor(gamma[:, :], VEC[:, V_QG:V_QG + HP], 1.0, gamma[:, :], ALU.add, ALU.mult)\
               .then_inc(consts_ready, 1)
            for k, (a, b, col) in enumerate(GROUPS):
                dve.wait_ge(setup_dma[k], 16)
                if col is None:
                    dve.tensor_copy(WH[:, a:b], stage[:, a:b]).then_inc(weights_hi, 1)
                    dve.wait_ge(weights_hi, k + 1)
                    last = dve.tensor_tensor(WL[:, a:b], stage[:, a:b], WH[:, a:b].bitcast(F32), ALU.subtract)
                else:
                    g = VEC[:, col:col + 1]
                    dve.tensor_scalar(WH[:, a:b], stage[:, a:b], g, None, ALU.mult).then_inc(weights_hi, 1)
                    dve.wait_ge(weights_hi, k + 1)
                    last = dve.scalar_tensor_tensor(WL[:, a:b], stage[:, a:b], g, WH[:, a:b].bitcast(F32),
                                                    ALU.mult, ALU.subtract)
            last.then_inc(weights_ready, 1)
            dve.wait_ge(consts_ready, 3)
            dve_steps = {
                "a_norm": a_norm, "a_turn": a_turn, "a_qk": a_qk, "a_scale": a_scale, "a_pairs": a_pairs,
                "a_values": a_values, "a_turn_out": a_turn_out, "a_out": a_out,
                "b_norm": b_norm, "f_turn_x": lambda i: split_xT(i, 0), "f_project": f_project, "f_scores": f_scores,
                "f_turn": f_turn, "f_values": f_values, "f_out": f_out, "f_norm": f_norm,
                "l_norm": l_norm, "l_turn_x": lambda i: split_xT(i, 2), "l_project": l_project, "l_scores": l_scores,
                "l_turn": l_turn, "l_values": l_values, "l_out": l_out, "l_norm2": l_norm2,
                "m_turn_x": lambda i, k: split_xT(i, mixtures[k].norm), "m_router": m_router, "m_top_a": m_top_a,
                "m_top_b": m_top_b, "m_top_c": m_top_c, "m_up": m_up, "m_down": m_down}
            passes(dve, dve_steps)
            assert all(c.links == c.per_unit for c in (chain_a, chain_x, chain_b, chain_n)), [c.links for c in (chain_a, chain_x, chain_b, chain_n)]


def kernel(**inputs):
    import numpy as np
    import concourse.bacc as _bacc
    from concourse import mybir as _mybir
    from concourse.bass_utils import run_bass_kernel_spmd as _run

    a = {k: np.asarray(v) for k, v in inputs.items()}

    def cols(w):
        w = w if w.ndim == 3 else w[None]
        return w.transpose(2, 0, 1).reshape(w.shape[2], -1)

    def rows(w):
        return w.reshape(-1, P, w.shape[1]).transpose(1, 0, 2).reshape(P, -1)

    wr = np.concatenate(
        [a["L0_attn_Wq"], a["L0_attn_Wkv"], cols(a["L0_ffn_Wq"])] + [cols(a["L0_ffn_Wkc"])] * FH
        + [cols(a["L0_ffn_Wvc"]), cols(a["L0_ffn_sW1"]), cols(a["L0_ffn_eW1"]), cols(a["L0_ffn_sW3"]),
           cols(a["L0_ffn_eW3"]), cols(a["L0_ffn_Wr"]), cols(a["L1_attn_Wq"]), cols(a["L1_attn_Wk"]),
           cols(a["L1_attn_Wv"]), cols(a["L1_ffn_Wr"]), cols(a["L1_ffn_W1"])], axis=1)
    w2 = a["L1_ffn_W2"]
    w2 = w2.reshape(w2.shape[0], w2.shape[1], J1, P).transpose(3, 0, 2, 1).reshape(P, -1)
    wf = np.concatenate([rows(a["L0_attn_Wo"]), cols(a["L0_ffn_Wo"]), cols(a["L0_ffn_sW2"]), cols(a["L0_ffn_eW2"]),
                         cols(a["L1_attn_Wo"]), w2], axis=1)
    everywhere = lambda v: np.broadcast_to(v[None, :], (P, v.shape[0]))
    vec = np.concatenate(
        [a["L0_attn_norm_w"][:, None], a["L0_ffn_g1"][:, None], a["L0_ffn_g2"][:, None], a["L1_attn_bq"][:, None],
         a["L1_attn_bk"][:, None], a["L0_attn_q_gamma"].reshape(HP, P).T, a["L0_attn_k_gamma"].reshape(HP, P).T,
         everywhere(a["L0_ffn_expert_bias"]), everywhere(a["L1_attn_bv"]), everywhere(a["L1_attn_bo"])], axis=1)
    named = {"x": a["L0_attn_tokens"], "wr": wr, "wf": wf, "vec": vec}

    nc = _bacc.Bacc("TRN2", target_bir_lowering=False, num_devices=1)
    arrays, args = {}, []
    for name, v in named.items():
        v = np.ascontiguousarray(v)
        arrays[f"in_{name}"] = v
        args.append(nc.dram_tensor(f"in_{name}", v.shape, _mybir.dt.from_np(v.dtype), kind="ExternalInput").ap())
    args.append(nc.dram_tensor("out_x", a["L0_attn_tokens"].shape, F32, kind="ExternalOutput").ap())
    program(nc, *args)
    r = _run(nc, [arrays], core_ids=[0])
    return r.results[0]["out_x"]
```

```python
from contextlib import ExitStack

import concourse.bass as bass
from concourse import mybir
from concourse.alu_op_type import AluOpType as ALU

F32 = mybir.dt.float32
F32R = mybir.dt.float32r
U32 = mybir.dt.uint32
ACT = mybir.ActivationFunctionType
AX_X = mybir.AxisListType.X

P = 128
D = 128
SEQ = 256
T = 4
N = T * P
H, DH = 16, 64
HP = H // 2
HALF = HP // 2
INNER = H * DH
CLAMP = 50.0
FH, FD = 4, 32
E0, E1 = 8, 8
J1 = 2
LN_EPS = 1e-5
RMS0_EPS = 1.1920928955078125e-07
RMS1_EPS = 1e-6

C_QK = 0
C_V = C_QK + 2 * INNER
C_FQ = C_V + INNER
C_FK = C_FQ + D
C_FV = C_FK + FH * FD
C_F1 = C_FV + FD
C_F3 = C_F1 + (E0 + 1) * D
C_FR = C_F3 + (E0 + 1) * D
C_LQ = C_FR + E0
C_LK = C_LQ + D
C_LV = C_LK + D
C_LR = C_LV + D
C_L1 = C_LR + E1
C_RSPLIT = C_L1 + E1 * 4 * D
C_WO = 0
C_FWO = C_WO + HP * D
C_F2 = C_FWO + D
C_LWO = C_F2 + (E0 + 1) * D
C_L2 = C_LWO + D
C_PLAIN = C_L2 + E1 * J1 * D
V_NW, V_G1, V_G2, V_BQ, V_BK, V_QG = 0, 1, 2, 3, 4, 5
V_KG = V_QG + HP
V_EB = V_KG + HP
V_BV = V_EB + E0
V_BO = V_BV + D
C_VEC = V_BO + D


def pieces(a, b, vector, count):
    step = (b - a) // count
    return [(a + k * step, a + (k + 1) * step, vector) for k in range(count)]


PIECES = (pieces(C_QK, C_FQ, V_NW, 3) + pieces(C_FQ, C_F1, V_G1, 1) + pieces(C_F1, C_LQ, V_G2, 2)
          + pieces(C_LQ, C_L1, None, 1) + pieces(C_L1, C_RSPLIT, None, 4))
A_PIECES = 3


ORDER = """
    a_qk:0,0,0 a_qk:0,0,1 f_turn_x a_qk:0,1,0 f_project f_scores:0 f_scores:1 f_turn:0 a_scale:0,0,0
    a_qk:0,1,1 f_values:0 a_v:0 f_scores:2 f_turn:1 a_v:1 f_values:1 f_scores:3 a_scale:0,0,1 f_turn:2
    a_scale:0,1,0 a_pairs:0,0,0 f_values:2 a_scale:0,1,1 a_pairs:0,0,1 f_turn:3 a_pairs:0,1,0 f_values:3
    a_pairs:0,1,1 f_turn_out f_out f_norm a_scores:0 a_norm:1 a_scores:1 a_scores:2 m_turn_x:0 a_values:0
    m_router:0 m_top_a:0 m_up:0,0 m_top_b:0 a_scores:3 a_values:1 m_up:0,1 a_scores:4 m_top_c:0 m_down:0,0
    m_up:0,2 a_values:2 a_scores:5 a_values:3 m_down:0,1 a_scores:6 m_up:0,3 m_down:0,2 a_values:4 m_up:0,4
    a_scores:7 m_down:0,3 a_centre:1 m_up:0,5 a_values:5 m_down:0,4 m_up:0,6 a_values:6 m_down:0,5 m_up:0,7
    m_down:0,6 m_up:0,8 a_values:7 m_down:0,7 a_turn:1 a_turn_out:0 a_turn_out:1 m_down:0,8 l_norm a_out:0
    a_qk:1,0,0 l_turn_x a_qk:1,0,1 a_qk:1,1,0 l_project a_scale:1,0,0 a_qk:1,1,1 l_scores:0 a_v:2 l_scores:1
    a_v:3 a_pairs:1,0,0 a_scale:1,0,1 l_theta:0 l_exp:0 a_pairs:1,0,1 l_theta:1 a_scale:1,1,0 l_turn:0
    a_scale:1,1,1 l_exp:1 l_values:0 l_turn:1 a_pairs:1,1,0 l_values:1 a_pairs:1,1,1 l_turn_out l_out
    a_scores:8 a_scores:9 l_norm2 a_scores:10 m_turn_x:1 a_values:8 m_router:1 m_top_a:1 m_up:1,0
    a_scores:11 a_values:9 m_top_b:1 m_up:1,1 m_top_c:1 a_scores:12 m_up:1,2 a_values:10 a_scores:13
    m_down:1,0 m_up:1,3 a_norm:0+ a_values:11 m_up:1,4 a_scores:14 m_up:1,5 m_down:1,1 m_up:1,6 a_values:12
    m_up:1,7 a_scores:15 m_down:1,2 m_up:1,8 a_values:13 m_up:1,9 m_down:1,3 m_up:1,10 m_down:1,4 m_up:1,11
    a_values:14 m_up:1,12 a_centre:0+ m_down:1,5 m_up:1,13 a_values:15 m_up:1,14 a_turn:0+ a_turn_out:2
    m_down:1,6 m_up:1,15 a_turn_out:3 a_out:1 b_norm+ m_down:1,7
"""


def step_of(text):
    name, _, args = text.rstrip("+").partition(":")
    ahead = int(name.startswith("a_")) + int(text.endswith("+"))
    return ahead, name, tuple(int(a) for a in args.split(",") if a)


PASS = [step_of(text) for text in ORDER.split()]
PLACE = {text: n for n, text in enumerate(ORDER.split())}
for before, after in (("f_values:3", "a_scores:1"), ("f_turn_out", "a_values:0"), ("a_out:0", "l_values:1"),
                      ("l_turn_out", f"a_scores:{HP + 1}"), ("f_out", "a_out:0"), ("a_out:1", "b_norm+")):
    assert PLACE[before] < PLACE[after], (before, after)
ALONE = [(i - 1, name, args) for i, name, args in PASS if i > 0]


def with_weights(steps):
    out = [(0, "weights", (0,)), (0, "a_norm", (0,)), (0, "a_centre", (0,)), (0, "a_turn", (0,)), (0, "weights", (1,))]
    for n, step in enumerate(steps):
        out.append(step)
        if n == 0:
            out.append((0, "weights", (2,)))
        if step[1] == "a_values" and step[2][0] + A_PIECES < len(PIECES):
            out.append((0, "weights", (step[2][0] + A_PIECES,)))
    return out


FIRST = with_weights(ALONE)
LAST_BUT_ONE = [step for step in PASS if step[0] < 2]
LAST = [step for step in PASS if step[0] == 0]
CHAIN_A, CHAIN_X, CHAIN_B, CHAIN_N = 24, 4, 37, 2


def program(nc, x, wr, wf, vec, out):
    UNITS = x.shape[0] * x.shape[1] // N
    assert UNITS > 2
    x_u = x.rearrange("b s d -> (b s) d").rearrange("(u t p) d -> u p t d", t=T, p=P)
    out_u = out.rearrange("b s d -> (b s) d").rearrange("(u t p) d -> u p t d", t=T, p=P)

    with ExitStack() as ctx:
        def sb(name, shape, dt=F32):
            return ctx.enter_context(nc.sbuf_tensor(name, shape, dt))

        def semaphore(name):
            return ctx.enter_context(nc.semaphore(name))

        class Signal:

            def __init__(self, name, per_unit, before=0):
                self.sem = semaphore(name)
                self.per_unit, self.before, self.links = per_unit, before, 0

            def at(self, i, k):
                return i * self.per_unit + (k + self.before)

        WH = sb("WH", [P, C_RSPLIT], F32R)
        WL = sb("WL", [P, C_RSPLIT], F32R)
        WF = sb("WF", [P, C_PLAIN])
        VEC = sb("VEC", [P, C_VEC])
        gamma = sb("gamma", [P, HP])
        ident = sb("ident", [P, P])
        half_neg = sb("half_neg", [P, 2 * H])
        iota8 = sb("iota8", [P, 8])
        A_COLS, B_COLS = 8192, 6144
        arena = sb("arena", [P, A_COLS + B_COLS])
        stage, at = [], {True: 0, False: A_COLS}
        for k, (a, b, _) in enumerate(PIECES):
            c0 = A_COLS if k == len(PIECES) - 1 else at[k < A_PIECES]
            at[k < A_PIECES] = c0 + (b - a)
            assert c0 + (b - a) <= A_COLS + B_COLS
            stage.append(arena[:, c0:c0 + (b - a)])

        raw = arena[:, 0:4096].rearrange("p (t n) -> p t n", t=2)
        ao = raw[:, :, 0:INNER]
        aoT = raw[:, :, INNER:2 * INNER]
        qT = arena[:, 4096:6144].rearrange("p (j n) -> p j n", j=HP)
        kT = arena[:, 6144:8192].rearrange("p (j n) -> p j n", j=HP)
        pT = sb("pT", [P, 3, 2, 2, SEQ])
        sq = pT[:, 0:2, :, :, :].rearrange("p a b c d -> p a (b c d)")
        vx = sb("vx", [P, 2, H, DH + 1])
        xin = sb("xin", [P, T, D])
        xn_a = sb("xn_a", [P, 2, D])
        xTh_a = sb("xTh_a", [P, SEQ], F32R)
        xTl_a = sb("xTl_a", [P, SEQ], F32R)
        stats_a = sb("stats_a", [P, 2, 6])
        mv_a = sb("mv_a", [P, 2, 2])
        parg_a = sb("parg_a", [P, 2])
        prs_a = sb("prs_a", [P, 2])
        ss = sb("ss", [P, 2, 2 * H])
        rn = sb("rn", [P, 2, 2 * H])
        rd_a = sb("rd_a", [P, 2, 4])
        xa = sb("xa", [P, T, D])

        def region(base, size):
            assert base + size <= B_COLS
            return arena[:, A_COLS + base:A_COLS + base + size]

        xr = sb("xr", [P, T, D])
        xl = sb("xl", [P, T, D])
        xn = sb("xn", [P, T, D])
        xTh = sb("xTh", [P, N], F32R)
        xTl = sb("xTl", [P, N], F32R)
        stats = sb("stats", [P, T, 6])
        mv = sb("mv", [P, T, 2])
        parg = sb("parg", [P, 2, T])
        prs = sb("prs", [P, 2, T])
        ms = sb("ms", [P, T])
        touch_a = sb("touch_a", [P, 2])
        touch_b = sb("touch_b", [P, 2])
        rd = sb("rd", [P, 4])
        nm = sb("nm", [P, 2, 4])
        idx8 = sb("idx8", [P, T, 8], U32)
        comb = sb("comb", [P, T, 8])
        fqz = sb("fqz", [P, FH, N])
        fv = sb("fv", [P, T, FD + 1])
        lv = sb("lv", [P, T, D + 1])
        fk = region(0, N)
        fp = region(3584, 2048).rearrange("p (s h k) -> p s h k", s=2, h=FH)
        fpT = region(512, 2048).rearrange("p (s m q) -> p s m q", s=2, m=2 * FH)
        fo = region(2560, N).rearrange("p (t d) -> p t d", t=T)
        foT = region(3072, N)
        lq, lk = region(0, N), region(512, N)
        ltheta = region(1024, 2 * N).rearrange("p (b n) -> p b n", b=2)
        lth = region(2048, 2 * N).rearrange("p (b n) -> p b n", b=2)
        lth2 = region(3072, 2 * N).rearrange("p (b n) -> p b n", b=2)
        lp = region(0, 2 * N).rearrange("p (t k) -> p t k", t=T)
        lpT = region(4096, 2 * N).rearrange("p (b m q) -> p b m q", b=2, m=4)
        lo = region(5120, N).rearrange("p (t d) -> p t d", t=T)
        loT = region(5632, N)
        th = region(0, 2 * N).rearrange("p (s n) -> p s n", s=2)
        gated = region(1024, 2 * N).rearrange("p (s n) -> p s n", s=2)
        hid = region(2048, 4 * N).rearrange("p (s n) -> p s n", s=4)
        small = region(4096, 12 * T * 8).rearrange("p (k n) -> p k n", k=12)

        PS = ctx.enter_context(nc.psum_tensor("PS", [P, 8, 512], F32))

        def bank(b, n=512):
            return PS[:, b, 0:n]

        def banks(b, k):
            return PS[:, b:b + k, :].rearrange("p b n -> p (b n)")

        SHARED, A_OUT, B_ONE, B_TWO = 2, 4, 5, 6

        setup_dma = [semaphore(f"setup_dma{k}") for k in range(len(PIECES) + 2)]
        ident_zero = semaphore("ident_zero")
        fqz_zero = semaphore("fqz_zero")
        ident_ready = semaphore("ident_ready")
        weights_hi = semaphore("weights_hi")
        weights_ready = semaphore("weights_ready")
        consts_ready = semaphore("consts_ready")
        x_loaded = Signal("x_loaded", 32)
        x_stored = Signal("x_stored", 16, before=16)
        chain_a = Signal("chain_a", CHAIN_A)
        chain_x = Signal("chain_x", CHAIN_X)
        chain_b = Signal("chain_b", CHAIN_B)
        chain_n = Signal("chain_n", CHAIN_N)
        a_pow_arg = Signal("a_pow_arg", 2)
        a_pow_done = Signal("a_pow_done", 2)
        a_xn = Signal("a_xn", 2)
        a_xT_psum = Signal("a_xT_psum", 2)
        a_xTh = Signal("a_xTh", 2)
        a_xT = Signal("a_xT", 2)
        qk_psum = Signal("qk_psum", 2 * T)
        v_psum = Signal("v_psum", T)
        raw_copied = Signal("raw_copied", 2 * T)
        v_copied = Signal("v_copied", T)
        squared = Signal("squared", 2 * T)
        ss_ready = Signal("ss_ready", 2 * T)
        rn_ready = Signal("rn_ready", 2 * T)
        qk_normed = Signal("qk_normed", 2 * T)
        pairs_psum = Signal("pairs_psum", 8)
        qT_ready = Signal("qT_ready", 4)
        kT_ready = Signal("kT_ready", 4)
        s_psum = Signal("s_psum", 2 * HP)
        tanh_done = Signal("tanh_done", 2 * HP)
        p_ready = Signal("p_ready", 2 * HP)
        o_psum = Signal("o_psum", 2 * HP)
        o_normed = Signal("o_normed", 2 * HP, before=1)
        aoT_psum = Signal("aoT_psum", T)
        aoT_act = Signal("aoT_act", T)
        aoT_dve = Signal("aoT_dve", T)
        wo_psum = Signal("wo_psum", 2)
        x_added = Signal("x_added", 2)
        b_pow_arg = Signal("b_pow_arg", 4)
        b_pow_done = Signal("b_pow_done", 4)
        b_xn = Signal("b_xn", 4)
        b_xT_psum = Signal("b_xT_psum", 4)
        b_xTh = Signal("b_xTh", 4)
        b_xT = Signal("b_xT", 4)
        f_proj = Signal("f_proj", 3)
        fq_ready = Signal("fq_ready", 1)
        fk_ready = Signal("fk_ready", 1)
        fv_ready = Signal("fv_ready", 1)
        f_scores_psum = Signal("f_scores_psum", T)
        f_max = Signal("f_max", T)
        f_p = Signal("f_p", T)
        f_pT_psum = Signal("f_pT_psum", T)
        f_pT_act = Signal("f_pT_act", T)
        f_pT_dve = Signal("f_pT_dve", T)
        f_o_psum = Signal("f_o_psum", T)
        f_o = Signal("f_o", T)
        f_oT_psum = Signal("f_oT_psum", 1)
        f_oT = Signal("f_oT", 1)
        f_wo = Signal("f_wo", 1)
        x2_ready = Signal("x2_ready", 1, before=1)
        x2_squares = Signal("x2_squares", 1)
        l_proj = Signal("l_proj", 3)
        lqk_ready = Signal("lqk_ready", 2)
        lv_ready = Signal("lv_ready", 1)
        l_scores_psum = Signal("l_scores_psum", 2)
        l_maps = Signal("l_maps", 2)
        l_theta = Signal("l_theta", 2)
        l_max = Signal("l_max", 2)
        l_p = Signal("l_p", 2)
        l_pT_psum = Signal("l_pT_psum", 2)
        l_pT_dve = Signal("l_pT_dve", 1)
        l_pT_act = Signal("l_pT_act", 1)
        l_o_psum = Signal("l_o_psum", 2)
        l_o = Signal("l_o", 2)
        l_oT_psum = Signal("l_oT_psum", 1)
        l_oT = Signal("l_oT", 1)
        l_wo = Signal("l_wo", 1)
        l_x = Signal("l_x", 1)
        l_xb = Signal("l_xb", 1)

        class Mixture:

            def __init__(self, tag, experts, parts, gate_col, value_col, down_col, router_col, shared, norm):
                self.experts, self.parts, self.shared, self.norm = experts, parts, shared, norm
                self.steps = experts * parts
                self.gate_col, self.value_col, self.down_col, self.router_col = gate_col, value_col, down_col, router_col
                self.router_psum = Signal(f"{tag}_router_psum", 1)
                self.logits_read = Signal(f"{tag}_logits_read", 1)
                self.router_max = Signal(f"{tag}_router_max", 1)
                self.router_exp = Signal(f"{tag}_router_exp", 1)
                self.top_diff = Signal(f"{tag}_top_diff", 1)
                self.top_exp = Signal(f"{tag}_top_exp", 1)
                self.gate_psum = Signal(f"{tag}_gate_psum", self.steps)
                self.value_psum = Signal(f"{tag}_value_psum", self.steps)
                self.th_ready = Signal(f"{tag}_th_ready", self.steps)
                self.gated_ready = Signal(f"{tag}_gated_ready", self.steps)
                self.hid_ready = Signal(f"{tag}_hid_ready", self.steps)
                self.y_psum = Signal(f"{tag}_y_psum", experts)
                self.y_added = Signal(f"{tag}_y_added", experts, before=1)

        mixtures = [
            Mixture("m0", E0 + 1, 1, lambda s: C_F1 + s * D, lambda s: C_F3 + s * D, lambda s: C_F2 + s * D,
                    C_FR, True, 1),
            Mixture("m1", E1, J1, lambda s: C_L1 + (s // J1 * 4 + J1 + s % J1) * D,
                    lambda s: C_L1 + (s // J1 * 4 + s % J1) * D, lambda s: C_L2 + s * D, C_LR, False, 3)]
        m0, m1 = mixtures

        def f_banks(t):
            return SHARED if t % 2 else B_TWO

        def f_out_bank(t):
            return A_OUT if t % 2 else B_ONE

        def l_bank(b):
            return SHARED if b else B_ONE


        def run(order, i, steps):
            for offset, name, args in order:
                if name in steps:
                    steps[name](i + offset, *args)

        def passes(engine, steps):
            run(FIRST, 0, steps)
            with engine.Fori(0, UNITS - 2) as i:
                run(PASS, i, steps)
            run(LAST_BUT_ONE, UNITS - 2, steps)
            run(LAST, UNITS - 1, steps)

        block = ctx.enter_context(nc.Block())

        @block.sync
        def _(sp):
            sp.dma_start(VEC[:, 0:V_BV], vec[:, 0:V_BV]).then_inc(setup_dma[-1], 16)
            for b in range(2):
                sp.dma_start(xin[:, 2 * b:2 * b + 2, :], x_u[0][:, 2 * b:2 * b + 2, :]).then_inc(x_loaded.sem, 16)
            sp.dma_start(VEC[:, V_BV:C_VEC], vec[:, V_BV:C_VEC]).then_inc(x_stored.sem, 16)
            for k, (a, b, _) in enumerate(PIECES):
                if k == len(PIECES) - 1:
                    sp.dma_start(WF[:, :], wf).then_inc(setup_dma[-2], 16)
                    sp.wait_ge(weights_ready, A_PIECES + 2)
                sp.dma_start(stage[k], wr[:, a:b]).then_inc(setup_dma[k], 16)

            def load(i):
                for b in range(2):
                    sp.wait_ge(x_added.sem, x_added.at(i - 1, b + 1))
                    sp.dma_start(xin[:, 2 * b:2 * b + 2, :], x_u[i][:, 2 * b:2 * b + 2, :]).then_inc(x_loaded.sem, 16)

            def store(i):
                sp.wait_ge(m1.y_added.sem, m1.y_added.at(i, m1.experts))
                sp.dma_start(out_u[i], xr[:, :, :]).then_inc(x_stored.sem, 16)

            load(1)
            with sp.Fori(0, UNITS - 2) as i:
                load(i + 2)
                store(i)
            store(UNITS - 2)
            store(UNITS - 1)
            sp.wait_ge(x_stored.sem, x_stored.at(UNITS, 0))

        @block.gpsimd
        def _(pool):
            pool.memset(ident[:, :], 0.0).then_inc(ident_zero, 1)
            pool.wait_ge(ident_zero, 1)
            pool.affine_select(out=ident[:, :], in_=ident[:, :], compare_op=ALU.not_equal, fill=1.0, base=0,
                               pattern=[[-1, P]], channel_multiplier=1).then_inc(ident_ready, 1)
            pool.wait_ge(consts_ready, 1)
            pool.wait_ge(x_stored.sem, 16)

            def a_norm(i, b):
                pool.wait_ge(a_pow_arg.sem, a_pow_arg.at(i, b + 1))
                pool.tensor_tensor(prs_a[:, :], parg_a[:, :], half_neg[:, 0:2], ALU.pow).then_inc(a_pow_done.sem, 1)

            def head_norms(i, b, part, t):
                pool.wait_ge(ss_ready.sem, ss_ready.at(i, 4 * b + 2 * part + t + 1))
                heads = slice(part * H, part * H + H)
                pool.tensor_tensor(rn[:, t, heads], ss[:, t, heads], half_neg[:, 0:H], ALU.pow).then_inc(rn_ready.sem, 1)

            def power(i, k):
                rows = 2 if k == 0 else 1
                pool.wait_ge(b_pow_arg.sem, b_pow_arg.at(i, k + 1))
                pool.tensor_tensor(prs[:, 0:rows, :].rearrange("p a t -> p (a t)"),
                                   parg[:, 0:rows, :].rearrange("p a t -> p (a t)"),
                                   half_neg[:, 0:rows * T], ALU.pow).then_inc(b_pow_done.sem, 1)

            def l_turn_x(i):
                pool.wait_ge(b_xn.sem, b_xn.at(i, 3))
                bo = VEC[:, V_BO:V_BO + D].unsqueeze(1).broadcast_to([P, T, D])
                pool.tensor_tensor(xl[:, :, :], xr[:, :, :], bo, ALU.add).then_inc(l_xb.sem, 1)

            passes(pool, {
                "a_norm": a_norm, "a_qk": head_norms, "l_turn_x": l_turn_x, "b_norm": lambda i: power(i, 0),
                "f_norm": lambda i: power(i, 1), "l_norm": lambda i: power(i, 2), "l_norm2": lambda i: power(i, 3)})

        @block.tensor
        def _(pe):
            def split_mm(dst, xh, xl, wh, wl, tokens_move, low_part=None):
                for x_part, w_part in ((xh, wh), (xh, wl), (xl, wh)):
                    if x_part is xl and low_part:
                        pe.wait_ge(*low_part)
                    stationary, moving = (w_part, x_part) if tokens_move else (x_part, w_part)
                    last = pe.matmul(dst, stationary, moving, start=w_part is wh and x_part is xh, stop=x_part is xl)
                return last

            def a_turn(i, b):
                pe.wait_ge(a_xn.sem, a_xn.at(i, b + 1))
                pe.wait_ge(o_normed.sem, o_normed.at(i, b * HP))
                for t in range(2):
                    last = pe.transpose(bank(A_OUT)[:, t * P:t * P + P], xn_a[:, t, :], ident[:, :])
                last.then_inc(a_xT_psum.sem, 1)

            def a_rows(t, col, low_part=None):
                c = slice(t * P, t * P + P)
                for q in range(2):
                    w = slice(col + 512 * q, col + 512 * q + 512)
                    last = split_mm(bank(q), xTh_a[:, c], xTl_a[:, c], WH[:, w], WL[:, w], False,
                                    None if q else low_part)
                return last

            def a_qk(i, b, part, t):
                low_part = None
                if part or t:
                    pe.wait_ge(raw_copied.sem, raw_copied.at(i, 4 * b + 2 * part + t))
                else:
                    pe.wait_ge(a_xTh.sem, a_xTh.at(i, b + 1))
                    low_part = (a_xT.sem, a_xT.at(i, b + 1))
                a_rows(t, C_QK + part * INNER, low_part).then_inc(qk_psum.sem, 1)

            def a_v(i, t):
                if t % 2:
                    pe.wait_ge(v_copied.sem, v_copied.at(i, t))
                else:
                    pe.wait_ge(raw_copied.sem, raw_copied.at(i, 2 * t + 4))
                a_rows(t % 2, C_V).then_inc(v_psum.sem, 1)

            def a_pairs(i, b, part, half):
                if part == 0 and half == 0:
                    pe.wait_ge(v_copied.sem, v_copied.at(i, 2 * b + 2))
                    pe.wait_ge(qk_normed.sem, qk_normed.at(i, 4 * b + 2))
                elif part == 0:
                    pe.wait_ge(qT_ready.sem, qT_ready.at(i, 2 * b + 1))
                elif half == 0:
                    pe.wait_ge(qT_ready.sem, qT_ready.at(i, 2 * b + 2))
                    pe.wait_ge(qk_normed.sem, qk_normed.at(i, 4 * b + 4))
                else:
                    pe.wait_ge(kT_ready.sem, kT_ready.at(i, 2 * b + 1))
                for n in range(HALF):
                    col = part * INNER + (half * HALF + n) * P
                    for t in range(2):
                        c0 = n % 2 * SEQ + t * P
                        last = pe.transpose(bank(n // 2)[:, c0:c0 + P], raw[:, t, col:col + P], ident[:, :])
                last.then_inc(pairs_psum.sem, 1)

            def a_scores(i, g):
                b, j, s = g // HP, g % HP, g % 2
                if j < 2:
                    pe.wait_ge(qT_ready.sem, qT_ready.at(i, 2 * b + 2))
                    pe.wait_ge(kT_ready.sem, kT_ready.at(i, 2 * b + 2))
                else:
                    pe.wait_ge(tanh_done.sem, tanh_done.at(i, g - 1))
                for kc in range(2):
                    for e in range(2):
                        rows = slice(e * DH, e * DH + DH)
                        last = pe.matmul(bank(2 * s + e)[:, kc * SEQ:kc * SEQ + SEQ], kT[rows, j, kc * P:kc * P + P],
                                         qT[rows, j, :], start=True, stop=True)
                last.then_inc(s_psum.sem, 1)

            def a_values(i, g):
                b, j = g // HP, g % HP
                pe.wait_ge(p_ready.sem, p_ready.at(i, g + 1))
                if j:
                    pe.wait_ge(o_normed.sem, o_normed.at(i, g))
                for qc in range(2):
                    for e in range(2):
                        c0 = (qc * 2 + e) * (DH + 1)
                        for kc in range(2):
                            last = pe.matmul(bank(A_OUT)[:, c0:c0 + DH + 1], pT[:, g % 3, e, kc, qc * P:qc * P + P],
                                             vx[:, kc, 2 * j + e, :], start=(kc == 0), stop=(kc == 1))
                last.then_inc(o_psum.sem, 1)

            def a_turn_out(i, t):
                b = t // 2
                if t % 2 == 0:
                    pe.wait_ge(o_normed.sem, o_normed.at(i, HP * (b + 1)))
                    pe.wait_ge(tanh_done.sem, tanh_done.at(i, HP * (b + 1)))
                for j in range(HP):
                    last = pe.transpose(bank(t % 2 * 2 + j // 4)[:, j % 4 * P:j % 4 * P + P],
                                        ao[:, t % 2, j * P:j * P + P], ident[:, :])
                last.then_inc(aoT_psum.sem, 1)

            def a_out(i, b):
                for t in (2 * b, 2 * b + 1):
                    pe.wait_ge(aoT_act.sem, aoT_act.at(i, t + 1))
                    pe.wait_ge(aoT_dve.sem, aoT_dve.at(i, t + 1))
                    for j in range(HP):
                        last = pe.matmul(bank(A_OUT)[:, t % 2 * D:t % 2 * D + D], aoT[:, t % 2, j * P:j * P + P],
                                         WF[:, C_WO + j * D:C_WO + j * D + D], start=(j == 0), stop=(j == HP - 1))
                last.then_inc(wo_psum.sem, 1)

            def w_T(dst, col, low_part=None):
                return split_mm(dst, xTh[:, :], xTl[:, :], WH[:, col:col + P], WL[:, col:col + P], True, low_part)

            def w_rows(dst, t, col, n, low_part=None):
                c = slice(t * P, t * P + P)
                return split_mm(dst, xTh[:, c], xTl[:, c], WH[:, col:col + n], WL[:, col:col + n], False, low_part)

            def turn_x(i, k):
                pe.wait_ge(b_xn.sem, b_xn.at(i, k + 1))
                if k == 0:
                    pe.wait_ge(m1.y_added.sem, m1.y_added.at(i, 0))
                for t in range(T):
                    last = pe.transpose(bank(B_ONE)[:, t * P:t * P + P], xn[:, t, :], ident[:, :])
                last.then_inc(b_xT_psum.sem, 1)

            def f_project(i):
                pe.wait_ge(b_xTh.sem, b_xTh.at(i, 1))
                w_T(bank(B_TWO), C_FQ, (b_xT.sem, b_xT.at(i, 1))).then_inc(f_proj.sem, 1)
                w_T(bank(B_TWO + 1), C_FK).then_inc(f_proj.sem, 1)
                for t in range(T):
                    last = w_rows(bank(B_ONE)[:, t * FD:t * FD + FD], t, C_FV, FD)
                last.then_inc(f_proj.sem, 1)

            def f_scores(i, t):
                if t == 0:
                    pe.wait_ge(fq_ready.sem, fq_ready.at(i, 1))
                    pe.wait_ge(fk_ready.sem, fk_ready.at(i, 1))
                elif t >= 2:
                    pe.wait_ge(f_pT_act.sem, f_pT_act.at(i, t - 1))
                    pe.wait_ge(f_pT_dve.sem, f_pT_dve.at(i, t - 1))
                k0 = t // 2 * SEQ
                for h in range(FH):
                    last = pe.matmul(bank(f_banks(t) + h // 2)[:, h % 2 * SEQ:h % 2 * SEQ + SEQ], fqz[:, h, t * P:t * P + P],
                                     fk[:, k0:k0 + SEQ], start=True, stop=True)
                last.then_inc(f_scores_psum.sem, 1)

            def f_turn(i, t):
                pe.wait_ge(f_p.sem, f_p.at(i, t + 1))
                for m in range(2 * FH):
                    last = pe.transpose(bank(f_banks(t) + m // 4)[:, m % 4 * P:m % 4 * P + P],
                                        fp[:, t % 2, m // 2, m % 2 * P:m % 2 * P + P], ident[:, :])
                last.then_inc(f_pT_psum.sem, 1)

            def f_values(i, t):
                pe.wait_ge(f_pT_act.sem, f_pT_act.at(i, t + 1))
                pe.wait_ge(f_pT_dve.sem, f_pT_dve.at(i, t + 1))
                if t == 0:
                    pe.wait_ge(fv_ready.sem, fv_ready.at(i, 1))
                elif t >= 2:
                    pe.wait_ge(f_o.sem, f_o.at(i, t - 1))
                for h in range(FH):
                    for kc in range(2):
                        last = pe.matmul(bank(f_out_bank(t))[:, h * (FD + 1):(h + 1) * (FD + 1)], fpT[:, t % 2, 2 * h + kc, :],
                                         fv[:, t // 2 * 2 + kc, :], start=(kc == 0), stop=(kc == 1))
                last.then_inc(f_o_psum.sem, 1)

            def f_turn_out(i):
                pe.wait_ge(f_o.sem, f_o.at(i, T))
                for t in range(T):
                    last = pe.transpose(bank(B_TWO)[:, t * P:t * P + P], fo[:, t, :], ident[:, :])
                last.then_inc(f_oT_psum.sem, 1)

            def f_out(i):
                pe.wait_ge(f_oT.sem, f_oT.at(i, 1))
                for t in range(T):
                    last = pe.matmul(bank(B_TWO + 1)[:, t * P:t * P + P], foT[:, t * P:t * P + P],
                                     WF[:, C_FWO:C_FWO + D], start=True, stop=True)
                last.then_inc(f_wo.sem, 1)

            def l_project(i):
                pe.wait_ge(b_xTh.sem, b_xTh.at(i, 3))
                w_T(bank(B_TWO), C_LQ, (b_xT.sem, b_xT.at(i, 3))).then_inc(l_proj.sem, 1)
                w_T(bank(B_TWO + 1), C_LK).then_inc(l_proj.sem, 1)
                for t in range(T):
                    last = w_rows(bank(B_ONE)[:, t * P:t * P + P], t, C_LV, D)
                last.then_inc(l_proj.sem, 1)

            def l_scores(i, b):
                if b == 0:
                    pe.wait_ge(lqk_ready.sem, lqk_ready.at(i, 2))
                for qc in range(2):
                    t = 2 * b + qc
                    last = pe.matmul(bank(B_TWO + b)[:, qc * SEQ:qc * SEQ + SEQ], lq[:, t * P:t * P + P],
                                     lk[:, b * SEQ:b * SEQ + SEQ], start=True, stop=True)
                last.then_inc(l_scores_psum.sem, 1)

            def l_turn(i, b):
                pe.wait_ge(l_p.sem, l_p.at(i, b + 1))
                for m in range(4):
                    qc, kc = m // 2, m % 2
                    last = pe.transpose(bank(B_TWO + b)[:, m * P:m * P + P], lp[:, 2 * b + qc, kc * P:kc * P + P],
                                        ident[:, :])
                last.then_inc(l_pT_psum.sem, 1)

            def l_values(i, b):
                if b == 0:
                    pe.wait_ge(lv_ready.sem, lv_ready.at(i, 1))
                    pe.wait_ge(l_pT_dve.sem, l_pT_dve.at(i, 1))
                else:
                    pe.wait_ge(l_pT_act.sem, l_pT_act.at(i, 1))
                for qc in range(2):
                    for kc in range(2):
                        last = pe.matmul(bank(l_bank(b))[:, qc * (D + 1):(qc + 1) * (D + 1)],
                                         lpT[:, b, 2 * qc + kc, :], lv[:, 2 * b + kc, :], start=(kc == 0), stop=(kc == 1))
                last.then_inc(l_o_psum.sem, 1)

            def l_turn_out(i):
                pe.wait_ge(l_o.sem, l_o.at(i, 2))
                for t in range(T):
                    last = pe.transpose(bank(B_TWO + 1)[:, t * P:t * P + P], lo[:, t, :], ident[:, :])
                last.then_inc(l_oT_psum.sem, 1)

            def l_out(i):
                pe.wait_ge(l_oT.sem, l_oT.at(i, 1))
                for t in range(T):
                    last = pe.matmul(bank(B_ONE)[:, t * P:t * P + P], loT[:, t * P:t * P + P], WF[:, C_LWO:C_LWO + D],
                                     start=True, stop=True)
                last.then_inc(l_wo.sem, 1)

            def m_router(i, k):
                m = mixtures[k]
                pe.wait_ge(b_xT.sem, b_xT.at(i, m.norm + 1))
                for t in range(T):
                    last = w_rows(bank(B_ONE)[:, t * 8:t * 8 + 8], t, m.router_col, 8)
                last.then_inc(m.router_psum.sem, 1)

            def m_up(i, k, s):
                m = mixtures[k]
                if s:
                    pe.wait_ge(m.gated_ready.sem, m.gated_ready.at(i, s))
                w_T(bank(B_TWO), m.gate_col(s)).then_inc(m.gate_psum.sem, 1)
                if s:
                    pe.wait_ge(m.hid_ready.sem, m.hid_ready.at(i, s))
                w_T(bank(B_TWO + 1), m.value_col(s)).then_inc(m.value_psum.sem, 1)

            def m_down(i, k, e):
                m = mixtures[k]
                pe.wait_ge(m.hid_ready.sem, m.hid_ready.at(i, (e + 1) * m.parts))
                if e:
                    pe.wait_ge(m.y_added.sem, m.y_added.at(i, e))
                else:
                    pe.wait_ge(m.logits_read.sem, m.logits_read.at(i, 1))
                for t in range(T):
                    for j in range(m.parts):
                        s = e * m.parts + j
                        last = pe.matmul(bank(B_ONE)[:, t * P:t * P + P], hid[:, s % 4, t * P:t * P + P],
                                         WF[:, m.down_col(s):m.down_col(s) + D], start=(j == 0), stop=(j == m.parts - 1))
                last.then_inc(m.y_psum.sem, 1)

            pe.wait_ge(ident_ready, 1)
            def weights(i, k):
                if k < A_PIECES or k == len(PIECES) - 1:
                    pe.wait_ge(weights_ready, k + 1)
                if k == len(PIECES) - 1:
                    pe.wait_ge(setup_dma[-2], 16)

            passes(pe, {
                "weights": weights,
                "a_turn": a_turn, "a_qk": a_qk, "a_v": a_v, "a_pairs": a_pairs, "a_scores": a_scores,
                "a_values": a_values, "a_turn_out": a_turn_out, "a_out": a_out,
                "f_turn_x": lambda i: turn_x(i, 0), "f_project": f_project, "f_scores": f_scores, "f_turn": f_turn,
                "f_values": f_values, "f_turn_out": f_turn_out, "f_out": f_out,
                "l_turn_x": lambda i: turn_x(i, 2), "l_project": l_project, "l_scores": l_scores, "l_turn": l_turn,
                "l_values": l_values, "l_turn_out": l_turn_out, "l_out": l_out,
                "m_turn_x": lambda i, k: turn_x(i, mixtures[k].norm), "m_router": m_router, "m_up": m_up,
                "m_down": m_down})

        @block.scalar
        def _(act):
            def a_qk(i, b, part, t):
                q = 4 * b + 2 * part + t
                features = raw[:, t, part * INNER:part * INNER + INNER]
                act.wait_ge(qk_psum.sem, qk_psum.at(i, q + 1))
                act.activation(features, banks(0, 2), ACT.Copy).then_inc(raw_copied.sem, 1)
                act.wait_ge(raw_copied.sem, raw_copied.at(i, q + 1))
                if q % 4 >= 2:
                    act.wait_ge(ss_ready.sem, ss_ready.at(i, q - 1))
                act.activation(sq[:, t, :], features, ACT.Square).then_inc(squared.sem, 1)

            def a_v(i, t):
                act.wait_ge(v_psum.sem, v_psum.at(i, t + 1))
                act.activation(vx[:, t % 2, :, 0:DH], banks(0, 2).rearrange("p (h d) -> p h d", h=H), ACT.Copy)\
                   .then_inc(v_copied.sem, 1)

            def a_pairs(i, b, part, half):
                if part == 0:
                    act.wait_ge(pairs_psum.sem, pairs_psum.at(i, 4 * b + half + 1))
                    act.activation(qT[:, half * HALF:(half + 1) * HALF, :].rearrange("p j n -> p (j n)"), banks(0, 2),
                                   ACT.Copy).then_inc(qT_ready.sem, 1)

            def exponent(i, g):
                act.wait_ge(tanh_done.sem, tanh_done.at(i, g + 1))
                v = pT[:, g % 3].rearrange("p a b c -> p (a b c)")
                act.activation(v, v, ACT.Exp, scale=CLAMP * DH ** -0.5).then_inc(p_ready.sem, 1)

            def a_scores(i, g):
                act.wait_ge(s_psum.sem, s_psum.at(i, g + 1))
                if g % HP == 0:
                    act.wait_ge(ss_ready.sem, ss_ready.at(i, 4 * (g // HP) + 4))
                if g % HP >= 3:
                    act.wait_ge(o_psum.sem, o_psum.at(i, g - 2))
                act.activation(pT[:, g % 3].rearrange("p a b c -> p (a b c)"), banks(2 * (g % 2), 2), ACT.Tanh,
                               scale=DH / CLAMP).then_inc(tanh_done.sem, 1)
                if g % HP:
                    exponent(i, g - 1)

            def a_values(i, g):
                if g % HP == HP - 2:
                    exponent(i, g + 1)

            def a_turn_out(i, t):
                act.wait_ge(aoT_psum.sem, aoT_psum.at(i, t + 1))
                act.activation(aoT[:, t % 2, 0:512], bank(t % 2 * 2), ACT.Copy).then_inc(aoT_act.sem, 1)

            def f_project(i):
                act.wait_ge(f_proj.sem, f_proj.at(i, 1))
                for h in range(FH):
                    rows = slice(h * FD, h * FD + FD)
                    last = act.activation(fqz[rows, h, :], bank(B_TWO)[rows, :], ACT.Copy, scale=FD ** -0.5)
                last.then_inc(fq_ready.sem, 1)

            def f_scores(i, t):
                act.wait_ge(f_max.sem, f_max.at(i, t + 1))
                if t >= 2:
                    act.wait_ge(f_pT_psum.sem, f_pT_psum.at(i, t - 1))
                for h in range(FH):
                    last = act.activation(fp[:, t % 2, h, :], bank(f_banks(t) + h // 2)[:, h % 2 * SEQ:h % 2 * SEQ + SEQ],
                                          ACT.Exp, bias=nm[:, t % 2, h:h + 1])
                last.then_inc(f_p.sem, 1)

            def f_turn(i, t):
                act.wait_ge(f_pT_psum.sem, f_pT_psum.at(i, t + 1))
                if t >= 2:
                    act.wait_ge(f_o_psum.sem, f_o_psum.at(i, t - 1))
                act.activation(fpT[:, t % 2, 0:4, :].rearrange("p m q -> p (m q)"), bank(f_banks(t)), ACT.Copy)\
                   .then_inc(f_pT_act.sem, 1)

            def f_turn_out(i):
                act.wait_ge(f_oT_psum.sem, f_oT_psum.at(i, 1))
                act.activation(foT, bank(B_TWO), ACT.Copy).then_inc(f_oT.sem, 1)

            def f_norm(i):
                act.wait_ge(x2_ready.sem, x2_ready.at(i, 1))
                for t in range(T):
                    last = act.activation(xn[:, t, :], xl[:, t, :], ACT.Square, accum_out=ms[:, t:t + 1])
                last.then_inc(x2_squares.sem, 1)

            def l_project(i):
                act.wait_ge(l_proj.sem, l_proj.at(i, 1))
                act.activation(lq, bank(B_TWO), ACT.Identity, bias=VEC[:, V_BQ:V_BQ + 1]).then_inc(lqk_ready.sem, 1)
                act.wait_ge(l_proj.sem, l_proj.at(i, 2))
                act.activation(lk, bank(B_TWO + 1), ACT.Identity, bias=VEC[:, V_BK:V_BK + 1]).then_inc(lqk_ready.sem, 1)

            def l_scores(i, b):
                act.wait_ge(l_scores_psum.sem, l_scores_psum.at(i, b + 1))
                act.activation(ltheta[:, b, :], bank(B_TWO + b), ACT.Relu)
                act.activation(lth[:, b, :], bank(B_TWO + b), ACT.Tanh, scale=0.5)
                act.activation(lth2[:, b, :], bank(B_TWO + b), ACT.Tanh).then_inc(l_maps.sem, 1)

            def l_exp(i, b):
                act.wait_ge(l_max.sem, l_max.at(i, b + 1))
                for qc in range(2):
                    last = act.activation(lp[:, 2 * b + qc, :], ltheta[:, b, qc * SEQ:qc * SEQ + SEQ], ACT.Exp,
                                          scale=0.1, bias=nm[:, b, 2 + qc:3 + qc])
                last.then_inc(l_p.sem, 1)

            def l_turn(i, b):
                if b == 0:
                    return
                act.wait_ge(l_pT_psum.sem, l_pT_psum.at(i, 2))
                act.activation(lpT[:, 1].rearrange("p m q -> p (m q)"), bank(B_TWO + 1), ACT.Copy).then_inc(l_pT_act.sem, 1)

            def l_turn_out(i):
                act.wait_ge(l_oT_psum.sem, l_oT_psum.at(i, 1))
                act.activation(loT, bank(B_TWO + 1), ACT.Copy).then_inc(l_oT.sem, 1)

            def m_top_a(i, k):
                m = mixtures[k]
                if m.shared:
                    act.wait_ge(m.router_max.sem, m.router_max.at(i, 1))
                    act.activation(small[:, 1, :], small[:, 0, :], ACT.Exp).then_inc(m.router_exp.sem, 1)

            def m_top_b(i, k):
                m = mixtures[k]
                act.wait_ge(m.top_diff.sem, m.top_diff.at(i, 1))
                act.activation(small[:, 5, 0:T], small[:, 4, 0:T], ACT.Exp).then_inc(m.top_exp.sem, 1)

            def m_up(i, k, s):
                m = mixtures[k]
                act.wait_ge(m.gate_psum.sem, m.gate_psum.at(i, s + 1))
                if s >= 2:
                    act.wait_ge(m.gated_ready.sem, m.gated_ready.at(i, s - 1))
                act.activation(th[:, s % 2, :], bank(B_TWO), ACT.Tanh, scale=0.5).then_inc(m.th_ready.sem, 1)

            act.wait_ge(setup_dma[-1], 16)
            act.wait_ge(fqz_zero, 1)
            passes(act, {
                "a_qk": a_qk, "a_v": a_v, "a_pairs": a_pairs, "a_scores": a_scores, "a_values": a_values,
                "a_turn_out": a_turn_out, "f_project": f_project, "f_scores": f_scores, "f_turn": f_turn,
                "f_turn_out": f_turn_out, "f_norm": f_norm, "l_project": l_project, "l_scores": l_scores,
                "l_exp": l_exp, "l_turn": l_turn, "l_turn_out": l_turn_out, "m_top_a": m_top_a, "m_top_b": m_top_b, "m_up": m_up})

        @block.vector
        def _(dve):
            def link(chain, i, ins):
                chain.links = chain.links % chain.per_unit + 1
                ins.then_inc(chain.sem, 1)
                dve.wait_ge(chain.sem, chain.at(i, chain.links))

            def moments(chain, i, dst, st, src, n, touch):
                for t in range(n):
                    last = dve.bn_stats(st[:, t, :], src[:, t, :])
                link(chain, i, last)
                dve.tensor_copy(touch[:, 1:2], touch[:, 0:1])
                for t in range(n):
                    last = dve.bn_aggr(dst[:, t, :], st[:, t, :])
                link(chain, i, last)

            def a_norm(i, b):
                dve.wait_ge(x_loaded.sem, x_loaded.at(i, 16 * (b + 1)))
                src = xin[:, 2 * b:2 * b + 2, :]
                moments(chain_x, i, mv_a, stats_a, src, 2, touch_a)
                dve.tensor_scalar(parg_a[:, :], mv_a[:, :, 1], 1.0 + RMS0_EPS, RMS0_EPS * LN_EPS, ALU.mult, ALU.add)\
                   .then_inc(a_pow_arg.sem, 1)

            def a_centre(i, b):
                src = xin[:, 2 * b:2 * b + 2, :]
                dve.wait_ge(a_pow_done.sem, a_pow_done.at(i, b + 1))
                for t in range(2):
                    last = dve.tensor_scalar(xn_a[:, t, :], src[:, t, :], mv_a[:, t, 0:1], prs_a[:, t:t + 1],
                                             ALU.subtract, ALU.mult)
                last.then_inc(a_xn.sem, 1)

            def a_turn(i, b):
                dve.wait_ge(a_xT_psum.sem, a_xT_psum.at(i, b + 1))
                dve.tensor_copy(xTh_a[:, :], bank(A_OUT, SEQ)).then_inc(a_xTh.sem, 1)
                dve.wait_ge(a_xTh.sem, a_xTh.at(i, b + 1))
                dve.tensor_tensor(xTl_a[:, :], bank(A_OUT, SEQ), xTh_a[:, :].bitcast(F32), ALU.subtract).then_inc(a_xT.sem, 1)

            def a_qk(i, b, part, t):
                q = 4 * b + 2 * part + t
                sums = ss[:, t, part * H:part * H + H]
                dve.wait_ge(squared.sem, squared.at(i, q + 1))
                link(chain_a, i, dve.tensor_reduce(sums, sq[:, t, :].rearrange("p (h d) -> p h d", d=DH), AX_X, ALU.add))
                dve.tensor_scalar(sums, sums, 1e-24, None, ALU.max).then_inc(ss_ready.sem, 1)

            def a_scale(i, b, part, t):
                dve.wait_ge(rn_ready.sem, rn_ready.at(i, 4 * b + 2 * part + t + 1))
                v = raw[:, t, part * INNER:part * INNER + INNER].rearrange("p (h d) -> p h d", d=DH)
                dve.tensor_tensor(v, v, rn[:, t, part * H:part * H + H].unsqueeze(2).broadcast_to([P, H, DH]), ALU.mult)\
                   .then_inc(qk_normed.sem, 1)

            def a_pairs(i, b, part, half):
                if part == 1:
                    js = slice(half * HALF, (half + 1) * HALF)
                    dve.wait_ge(pairs_psum.sem, pairs_psum.at(i, 4 * b + 2 + half + 1))
                    dve.tensor_tensor(kT[:, js, :], banks(0, 2).rearrange("p (j n) -> p j n", j=HALF),
                                      gamma[:, js].unsqueeze(2).broadcast_to([P, HALF, SEQ]), ALU.mult)\
                       .then_inc(kT_ready.sem, 1)

            def a_values(i, g):
                j = g % HP
                o = bank(A_OUT, 4 * (DH + 1)).rearrange("p (m d) -> p m d", d=DH + 1)
                dve.wait_ge(o_psum.sem, o_psum.at(i, g + 1))
                link(chain_a, i, dve.reciprocal(rd_a[:, g % 2, :], o[:, :, DH]))
                dve.tensor_tensor(ao[:, :, j * P:j * P + P].rearrange("p q (e d) -> p q e d", e=2),
                                  o[:, :, 0:DH].rearrange("p (q e) d -> p q e d", e=2),
                                  rd_a[:, g % 2, :].rearrange("p (q e) -> p q e", e=2).unsqueeze(3).broadcast_to([P, 2, 2, DH]),
                                  ALU.mult).then_inc(o_normed.sem, 1)

            def a_turn_out(i, t):
                dve.wait_ge(aoT_psum.sem, aoT_psum.at(i, t + 1))
                dve.tensor_copy(aoT[:, t % 2, 512:1024], bank(t % 2 * 2 + 1)).then_inc(aoT_dve.sem, 1)

            def a_out(i, b):
                dve.wait_ge(wo_psum.sem, wo_psum.at(i, b + 1))
                if b == 0:
                    dve.wait_ge(x2_ready.sem, x2_ready.at(i, 0))
                dve.tensor_tensor(xa[:, 2 * b:2 * b + 2, :], xin[:, 2 * b:2 * b + 2, :],
                                  bank(A_OUT, SEQ).rearrange("p (t d) -> p t d", t=2), ALU.add).then_inc(x_added.sem, 1)

            def centre(dst, src, row):
                for t in range(T):
                    last = dve.tensor_scalar(dst[:, t, :], src[:, t, :], mv[:, t, 0:1], prs[:, row, t:t + 1],
                                             ALU.subtract, ALU.mult)
                return last

            def split_xT(i, k):
                dve.wait_ge(b_xT_psum.sem, b_xT_psum.at(i, k + 1))
                dve.tensor_copy(xTh[:, :], bank(B_ONE)).then_inc(b_xTh.sem, 1)
                dve.wait_ge(b_xTh.sem, b_xTh.at(i, k + 1))
                dve.tensor_tensor(xTl[:, :], bank(B_ONE), xTh[:, :].bitcast(F32), ALU.subtract).then_inc(b_xT.sem, 1)

            def b_norm(i):
                dve.wait_ge(x_added.sem, x_added.at(i, 2))
                moments(chain_n, i, mv, stats, xa, T, touch_b)
                dve.tensor_scalar(parg[:, 0, :], mv[:, :, 1], 1.0 + RMS1_EPS, RMS1_EPS * LN_EPS, ALU.mult, ALU.add)
                dve.tensor_scalar(parg[:, 1, :], mv[:, :, 1], LN_EPS, None, ALU.add).then_inc(b_pow_arg.sem, 1)
                dve.wait_ge(b_pow_done.sem, b_pow_done.at(i, 1))
                centre(xn, xa, 0).then_inc(b_xn.sem, 1)
                centre(xl, xa, 1)

            def f_project(i):
                dve.wait_ge(f_proj.sem, f_proj.at(i, 2))
                dve.tensor_copy(fk, bank(B_TWO + 1)).then_inc(fk_ready.sem, 1)
                dve.wait_ge(f_proj.sem, f_proj.at(i, 3))
                dve.tensor_copy(fv[:, :, 0:FD], bank(B_ONE, T * FD).rearrange("p (t d) -> p t d", t=T))\
                   .then_inc(fv_ready.sem, 1)

            def f_scores(i, t):
                dve.wait_ge(f_scores_psum.sem, f_scores_psum.at(i, t + 1))
                dve.tensor_reduce(nm[:, t % 2, :], banks(f_banks(t), 2).rearrange("p (h k) -> p h k", h=FH),
                                  AX_X, ALU.max, negate=True).then_inc(f_max.sem, 1)

            def f_turn(i, t):
                dve.wait_ge(f_pT_psum.sem, f_pT_psum.at(i, t + 1))
                if t >= 2:
                    dve.wait_ge(f_o_psum.sem, f_o_psum.at(i, t - 1))
                dve.tensor_copy(fpT[:, t % 2, 4:8, :].rearrange("p m q -> p (m q)"), bank(f_banks(t) + 1))\
                   .then_inc(f_pT_dve.sem, 1)

            def f_values(i, t):
                o = bank(f_out_bank(t), FH * (FD + 1)).rearrange("p (h d) -> p h d", h=FH)
                dve.wait_ge(f_o_psum.sem, f_o_psum.at(i, t + 1))
                link(chain_b, i, dve.reciprocal(rd[:, :], o[:, :, FD]))
                dve.tensor_tensor(fo[:, t, :].rearrange("p (h d) -> p h d", h=FH), o[:, :, 0:FD],
                                  rd[:, :].unsqueeze(2).broadcast_to([P, FH, FD]), ALU.mult).then_inc(f_o.sem, 1)

            def f_out(i):
                dve.wait_ge(f_wo.sem, f_wo.at(i, 1))
                dve.wait_ge(x_stored.sem, x_stored.at(i, 0))
                rows = bank(B_TWO + 1).rearrange("p (t d) -> p t d", t=T)
                link(chain_b, i, dve.tensor_tensor(xl[:, :, :], xl[:, :, :], rows, ALU.add))
                dve.tensor_tensor(xr[:, :, :], xa[:, :, :], xl[:, :, :], ALU.add).then_inc(x2_ready.sem, 1)

            def f_norm(i):
                dve.wait_ge(x2_squares.sem, x2_squares.at(i, 1))
                dve.tensor_scalar(parg[:, 0, :], ms[:, :], 1.0 / D, RMS1_EPS, ALU.mult, ALU.add).then_inc(b_pow_arg.sem, 1)
                dve.wait_ge(b_pow_done.sem, b_pow_done.at(i, 2))
                for t in range(T):
                    last = dve.tensor_scalar(xn[:, t, :], xl[:, t, :], prs[:, 0, t:t + 1], None, ALU.mult)
                last.then_inc(b_xn.sem, 1)

            def norm_xr(i, k):
                moments(chain_b, i, mv, stats, xr, T, touch_b)
                dve.tensor_scalar(parg[:, 0, :], mv[:, :, 1], LN_EPS, None, ALU.add).then_inc(b_pow_arg.sem, 1)
                dve.wait_ge(b_pow_done.sem, b_pow_done.at(i, k + 1))
                centre(xn, xr, 0).then_inc(b_xn.sem, 1)

            def l_norm(i):
                dve.wait_ge(m0.y_added.sem, m0.y_added.at(i, m0.experts))
                norm_xr(i, 2)

            def l_project(i):
                dve.wait_ge(l_proj.sem, l_proj.at(i, 3))
                bv = VEC[:, V_BV:V_BV + D].unsqueeze(1).broadcast_to([P, T, D])
                dve.tensor_tensor(lv[:, :, 0:D], bank(B_ONE).rearrange("p (t d) -> p t d", t=T), bv, ALU.add)\
                   .then_inc(lv_ready.sem, 1)

            def l_theta_of(i, b):
                dve.wait_ge(l_maps.sem, l_maps.at(i, b + 1))
                link(chain_b, i, dve.scalar_tensor_tensor(ltheta[:, b, :], lth[:, b, :], 6.0, ltheta[:, b, :], ALU.add, ALU.add))
                dve.scalar_tensor_tensor(ltheta[:, b, :], lth2[:, b, :], 1.5, ltheta[:, b, :], ALU.mult, ALU.add)\
                   .then_inc(l_theta.sem, 1)
                dve.wait_ge(l_theta.sem, l_theta.at(i, b + 1))
                link(chain_b, i, dve.tensor_reduce(nm[:, b, 0:2], ltheta[:, b, :].rearrange("p (q k) -> p q k", q=2),
                                                   AX_X, ALU.max, negate=True))
                dve.tensor_scalar(nm[:, b, 2:4], nm[:, b, 0:2], 0.1, None, ALU.mult).then_inc(l_max.sem, 1)

            def l_turn(i, b):
                if b:
                    return
                dve.wait_ge(l_pT_psum.sem, l_pT_psum.at(i, 1))
                dve.tensor_copy(lpT[:, 0].rearrange("p m q -> p (m q)"), bank(B_TWO)).then_inc(l_pT_dve.sem, 1)

            def l_values(i, b):
                o = bank(l_bank(b), 2 * (D + 1)).rearrange("p (q d) -> p q d", q=2)
                dve.wait_ge(l_o_psum.sem, l_o_psum.at(i, b + 1))
                link(chain_b, i, dve.reciprocal(rd[:, 2 * b:2 * b + 2], o[:, :, D]))
                dve.tensor_tensor(lo[:, 2 * b:2 * b + 2, :], o[:, :, 0:D],
                                  rd[:, 2 * b:2 * b + 2].unsqueeze(2).broadcast_to([P, 2, D]), ALU.mult)\
                   .then_inc(l_o.sem, 1)

            def l_out(i):
                dve.wait_ge(l_wo.sem, l_wo.at(i, 1))
                dve.wait_ge(l_xb.sem, l_xb.at(i, 1))
                dve.tensor_tensor(xr[:, :, :], xl[:, :, :], bank(B_ONE).rearrange("p (t d) -> p t d", t=T), ALU.add)\
                   .then_inc(l_x.sem, 1)

            def l_norm2(i):
                dve.wait_ge(l_x.sem, l_x.at(i, 1))
                norm_xr(i, 3)

            def experts_of(row):
                return small[:, row, :].rearrange("p (t e) -> p t e", t=T)

            def per_token(row):
                return small[:, row, 0:T].unsqueeze(2).broadcast_to([P, T, 8])

            def m_router(i, k):
                m = mixtures[k]
                logits = bank(B_ONE, T * 8)
                dve.wait_ge(m.router_psum.sem, m.router_psum.at(i, 1))
                if m.shared:
                    eb = VEC[:, V_EB:V_EB + 8].unsqueeze(1).broadcast_to([P, T, 8])
                    dve.tensor_tensor(experts_of(0), logits.rearrange("p (t e) -> p t e", t=T), eb, ALU.add)\
                       .then_inc(m.logits_read.sem, 1)
                    dve.wait_ge(m.logits_read.sem, m.logits_read.at(i, 1))
                    link(chain_b, i, dve.tensor_reduce(small[:, 6, 0:T], experts_of(0), AX_X, ALU.max))
                    dve.tensor_tensor(experts_of(0), experts_of(0), per_token(6), ALU.subtract).then_inc(m.router_max.sem, 1)
                else:
                    dve.tensor_copy(small[:, 2, :], logits).then_inc(m.logits_read.sem, 1)

            def m_top_a(i, k):
                m = mixtures[k]
                if m.shared:
                    dve.wait_ge(m.router_exp.sem, m.router_exp.at(i, 1))
                    link(chain_b, i, dve.tensor_reduce(small[:, 7, 0:T], experts_of(1), AX_X, ALU.add))
                    link(chain_b, i, dve.reciprocal(small[:, 8, 0:T], small[:, 7, 0:T]))
                    link(chain_b, i, dve.tensor_tensor(experts_of(2), experts_of(1), per_token(8), ALU.mult))
                else:
                    dve.wait_ge(m.logits_read.sem, m.logits_read.at(i, 1))
                dve.tensor_copy(touch_b[:, 1:2], touch_b[:, 0:1])
                for t in range(T):
                    last = dve.max(experts_of(3)[:, t, :], experts_of(2)[:, t, :])
                link(chain_b, i, last)
                dve.tensor_tensor(small[:, 4, 0:T], experts_of(3)[:, :, 1], experts_of(3)[:, :, 0], ALU.subtract)\
                   .then_inc(m.top_diff.sem, 1)
                for t in range(T):
                    last = dve.max_index(idx8[:, t, :], experts_of(3)[:, t, :], experts_of(2)[:, t, :])
                link(chain_b, i, last)
                link(chain_b, i, dve.tensor_copy(experts_of(9), idx8[:, :, :]))

            def m_top_b(i, k):
                lane = iota8[:, :].unsqueeze(1).broadcast_to([P, T, 8])
                for n in range(2):
                    last = dve.tensor_tensor(experts_of(10 + n), lane, experts_of(9)[:, :, n:n + 1].broadcast_to([P, T, 8]),
                                             ALU.is_equal)
                link(chain_b, i, last)

            def m_top_c(i, k):
                m = mixtures[k]
                dve.wait_ge(m.top_exp.sem, m.top_exp.at(i, 1))
                link(chain_b, i, dve.tensor_scalar(small[:, 6, 0:T], small[:, 5, 0:T], 2.0, 2.0, ALU.mult, ALU.add))
                link(chain_b, i, dve.reciprocal(small[:, 7, 0:T], small[:, 6, 0:T]))
                link(chain_b, i, dve.tensor_tensor(small[:, 8, 0:T], small[:, 7, 0:T], small[:, 5, 0:T], ALU.mult))
                for n in range(2):
                    last = dve.tensor_tensor(experts_of(10 + n), experts_of(10 + n), per_token(7 + n), ALU.mult)
                link(chain_b, i, last)
                link(chain_b, i, dve.tensor_tensor(comb[:, :, :], experts_of(10), experts_of(11), ALU.add))

            def m_up(i, k, s):
                m = mixtures[k]
                dve.wait_ge(m.th_ready.sem, m.th_ready.at(i, s + 1))
                dve.scalar_tensor_tensor(gated[:, s % 2, :], th[:, s % 2, :], 1.0, bank(B_TWO), ALU.add, ALU.mult)\
                   .then_inc(m.gated_ready.sem, 1)
                dve.wait_ge(m.gated_ready.sem, m.gated_ready.at(i, s + 1))
                dve.wait_ge(m.value_psum.sem, m.value_psum.at(i, s + 1))
                if s >= 4:
                    dve.wait_ge(m.y_psum.sem, m.y_psum.at(i, (s - 4) // m.parts + 1))
                dve.tensor_tensor(hid[:, s % 4, :], gated[:, s % 2, :], bank(B_TWO + 1), ALU.mult)\
                   .then_inc(m.hid_ready.sem, 1)

            def m_down(i, k, e):
                m = mixtures[k]
                dve.wait_ge(m.y_psum.sem, m.y_psum.at(i, e + 1))
                if e:
                    dve.wait_ge(m.y_added.sem, m.y_added.at(i, e))
                y = bank(B_ONE)
                if m.shared and e == 0:
                    flat = xr[:, :, :].rearrange("p t d -> p (t d)")
                    last = dve.scalar_tensor_tensor(flat, y, 0.5, flat, ALU.mult, ALU.add)
                else:
                    c = e - 1 if m.shared else e
                    for t in range(T):
                        last = dve.scalar_tensor_tensor(xr[:, t, :], y[:, t * P:t * P + P], comb[:, t, c:c + 1],
                                                        xr[:, t, :], ALU.mult, ALU.add)
                last.then_inc(m.y_added.sem, 1)

            dve.memset(half_neg[:, :], -0.5).then_inc(consts_ready, 1)
            dve.memset(vx[:, :, :, DH:DH + 1], 1.0).then_inc(o_normed.sem, 1)
            dve.memset(fqz[:, :, :], 0.0).then_inc(fqz_zero, 1)
            dve.memset(fv[:, :, FD:FD + 1], 1.0)
            dve.memset(lv[:, :, D:D + 1], 1.0)
            dve.memset(touch_a[:, :], 1.0).then_inc(x2_ready.sem, 1)
            dve.memset(touch_b[:, :], 1.0).then_inc(m1.y_added.sem, 1)
            dve.memset(comb[:, :, :], 0.0).then_inc(m0.y_added.sem, 1)
            for e in range(8):
                dve.memset(iota8[:, e:e + 1], float(e))
            dve.wait_ge(setup_dma[-1], 16)
            dve.tensor_scalar(gamma[:, :], VEC[:, V_KG:V_KG + HP], 1.0, None, ALU.add).then_inc(consts_ready, 1)
            dve.wait_ge(consts_ready, 2)
            dve.scalar_tensor_tensor(gamma[:, :], VEC[:, V_QG:V_QG + HP], 1.0, gamma[:, :], ALU.add, ALU.mult)\
               .then_inc(consts_ready, 1)
            def weights(i, k):
                a, b, col = PIECES[k]
                dve.wait_ge(setup_dma[k], 16)
                if col is None:
                    dve.tensor_copy(WH[:, a:b], stage[k]).then_inc(weights_hi, 1)
                    dve.wait_ge(weights_hi, k + 1)
                    last = dve.tensor_tensor(WL[:, a:b], stage[k], WH[:, a:b].bitcast(F32), ALU.subtract)
                else:
                    g = VEC[:, col:col + 1]
                    dve.tensor_scalar(WH[:, a:b], stage[k], g, None, ALU.mult).then_inc(weights_hi, 1)
                    dve.wait_ge(weights_hi, k + 1)
                    last = dve.scalar_tensor_tensor(WL[:, a:b], stage[k], g, WH[:, a:b].bitcast(F32),
                                                    ALU.mult, ALU.subtract)
                last.then_inc(weights_ready, 1)

            dve.wait_ge(consts_ready, 3)
            dve_steps = {
                "weights": weights,
                "a_norm": a_norm, "a_centre": a_centre, "a_turn": a_turn, "a_qk": a_qk, "a_scale": a_scale, "a_pairs": a_pairs,
                "a_values": a_values, "a_turn_out": a_turn_out, "a_out": a_out,
                "b_norm": b_norm, "f_turn_x": lambda i: split_xT(i, 0), "f_project": f_project, "f_scores": f_scores,
                "f_turn": f_turn, "f_values": f_values, "f_out": f_out, "f_norm": f_norm,
                "l_norm": l_norm, "l_turn_x": lambda i: split_xT(i, 2), "l_project": l_project, "l_theta": l_theta_of,
                "l_turn": l_turn, "l_values": l_values, "l_out": l_out, "l_norm2": l_norm2,
                "m_turn_x": lambda i, k: split_xT(i, mixtures[k].norm), "m_router": m_router, "m_top_a": m_top_a,
                "m_top_b": m_top_b, "m_top_c": m_top_c, "m_up": m_up, "m_down": m_down}
            passes(dve, dve_steps)
            assert all(c.links == c.per_unit for c in (chain_a, chain_x, chain_b, chain_n))


def kernel(**inputs):
    import numpy as np
    import concourse.bacc as _bacc
    from concourse import mybir as _mybir
    from concourse.bass_utils import run_bass_kernel_spmd as _run

    a = {k: np.asarray(v) for k, v in inputs.items()}

    def cols(w):
        w = w if w.ndim == 3 else w[None]
        return w.transpose(2, 0, 1).reshape(w.shape[2], -1)

    def rows(w):
        return w.reshape(-1, P, w.shape[1]).transpose(1, 0, 2).reshape(P, -1)

    wr = np.concatenate(
        [a["L0_attn_Wq"], a["L0_attn_Wkv"], cols(a["L0_ffn_Wq"])] + [cols(a["L0_ffn_Wkc"])] * FH
        + [cols(a["L0_ffn_Wvc"]), cols(a["L0_ffn_sW1"]), cols(a["L0_ffn_eW1"]), cols(a["L0_ffn_sW3"]),
           cols(a["L0_ffn_eW3"]), cols(a["L0_ffn_Wr"]), cols(a["L1_attn_Wq"]), cols(a["L1_attn_Wk"]),
           cols(a["L1_attn_Wv"]), cols(a["L1_ffn_Wr"]), cols(a["L1_ffn_W1"])], axis=1)
    w2 = a["L1_ffn_W2"]
    w2 = w2.reshape(w2.shape[0], w2.shape[1], J1, P).transpose(3, 0, 2, 1).reshape(P, -1)
    wf = np.concatenate([rows(a["L0_attn_Wo"]), cols(a["L0_ffn_Wo"]), cols(a["L0_ffn_sW2"]), cols(a["L0_ffn_eW2"]),
                         cols(a["L1_attn_Wo"]), w2], axis=1)
    everywhere = lambda v: np.broadcast_to(v[None, :], (P, v.shape[0]))
    vec = np.concatenate(
        [a["L0_attn_norm_w"][:, None], a["L0_ffn_g1"][:, None], a["L0_ffn_g2"][:, None], a["L1_attn_bq"][:, None],
         a["L1_attn_bk"][:, None], a["L0_attn_q_gamma"].reshape(HP, P).T, a["L0_attn_k_gamma"].reshape(HP, P).T,
         everywhere(a["L0_ffn_expert_bias"]), everywhere(a["L1_attn_bv"]), everywhere(a["L1_attn_bo"])], axis=1)
    named = {"x": a["L0_attn_tokens"], "wr": wr, "wf": wf, "vec": vec}

    nc = _bacc.Bacc("TRN2", target_bir_lowering=False, num_devices=1)
    arrays, args = {}, []
    for name, v in named.items():
        v = np.ascontiguousarray(v)
        arrays[f"in_{name}"] = v
        args.append(nc.dram_tensor(f"in_{name}", v.shape, _mybir.dt.from_np(v.dtype), kind="ExternalInput").ap())
    args.append(nc.dram_tensor("out_x", a["L0_attn_tokens"].shape, F32, kind="ExternalOutput").ap())
    program(nc, *args)
    r = _run(nc, [arrays], core_ids=[0])
    return r.results[0]["out_x"]
```
